# Optimizing a Trainium2 kernel written in Bass

```python
import numpy as np
import jax
import jax.numpy as jnp

def _softmax(x, axis=-1):
    return jax.nn.softmax(x, axis=axis)

def _gelu(x):
    return jax.nn.gelu(x, approximate=True)

def _silu(x):
    return jax.nn.silu(x)

def _sigmoid(x):
    return jax.nn.sigmoid(x)

def _layernorm(x, axis=-1, eps=1e-05):
    m = jnp.mean(x, axis=axis, keepdims=True)
    v = jnp.var(x, axis=axis, keepdims=True)
    return (x - m) / jnp.sqrt(v + eps)

def _scatter_add(tgt, idx, src, axis=0):
    return tgt.at[idx].add(src)

def _segment_sum(src, seg, n):
    return jax.ops.segment_sum(src, seg, n)
kernel_name = 'mk_adj_resnorm_d1_adj_r2_10e70f'

def setup_inputs(seed: int=0):
    np.random.seed(seed)
    _w = jnp.asarray

    def _rec_inputs():
        import jax
        import jax.numpy as jnp
        _gk = jax.random.key(seed)
        x = 7.22e-05 + 1 * jax.random.normal(jax.random.fold_in(_gk, 1), (64, 128, 256), jnp.float32)
        _a = jax.random.bernoulli(jax.random.fold_in(_gk, 2), 0.125, (128, 128))
        _a = jnp.logical_or(_a, jnp.swapaxes(_a, -1, -2))
        _a = jnp.logical_or(_a, jnp.eye(128, dtype=bool))
        _af = _a.astype(jnp.float32)
        _af = _af * jax.random.uniform(jax.random.fold_in(_gk, 3), (128, 128), jnp.float32, 0.05, 0.00390622)
        adj = _af
        return (x, adj)
    x, adj = _rec_inputs()

    def _L0_gnn_setup():
        import jax, jax.numpy as jnp
        import numpy as np
        B, N, D, T = (64, 128, 256, 3)

        def _lin(v, W, b):
            return jnp.einsum('...i,oi->...o', v, W) + b
        key = jax.random.key(seed)
        ks = jax.random.split(key, 12)
        s2 = 1.0 / np.sqrt(2 * D)
        s1 = 1.0 / np.sqrt(D)
        return {'x': jax.random.normal(ks[0], (B, N, D), jnp.float32), 'in_mat': jax.random.uniform(ks[1], (N, N), jnp.float32) / N, 'out_mat': jax.random.uniform(ks[2], (N, N), jnp.float32) / N, 'w3_w': jax.random.normal(ks[3], (D, 2 * D), jnp.float32) * s2, 'w3_b': jnp.zeros((D,), jnp.float32), 'u3_w': jax.random.normal(ks[4], (D, D), jnp.float32) * s1, 'u3_b': jnp.zeros((D,), jnp.float32), 'w4_w': jax.random.normal(ks[5], (D, 2 * D), jnp.float32) * s2, 'w4_b': jnp.zeros((D,), jnp.float32), 'w5_w': jax.random.normal(ks[6], (D, 2 * D), jnp.float32) * s2, 'w5_b': jnp.zeros((D,), jnp.float32), 'u5_w': jax.random.normal(ks[7], (D, D), jnp.float32) * s1, 'u5_b': jnp.zeros((D,), jnp.float32)}
    _L0_gnn_all = _L0_gnn_setup()
    _L0_gnn_in = {k: v for k, v in _L0_gnn_all.items() if k in ('w3_w', 'w3_b', 'u3_w', 'u3_b', 'w4_w', 'w4_b', 'w5_w', 'w5_b', 'u5_w', 'u5_b')}
    del _L0_gnn_all
    return {'x': x, 'adj': adj, 'L0_gnn_w3_w': _L0_gnn_in['w3_w'], 'L0_gnn_w3_b': _L0_gnn_in['w3_b'], 'L0_gnn_u3_w': _L0_gnn_in['u3_w'], 'L0_gnn_u3_b': _L0_gnn_in['u3_b'], 'L0_gnn_w4_w': _L0_gnn_in['w4_w'], 'L0_gnn_w4_b': _L0_gnn_in['w4_b'], 'L0_gnn_w5_w': _L0_gnn_in['w5_w'], 'L0_gnn_w5_b': _L0_gnn_in['w5_b'], 'L0_gnn_u5_w': _L0_gnn_in['u5_w'], 'L0_gnn_u5_b': _L0_gnn_in['u5_b']}

def reference(x, adj, L0_gnn_w3_w, L0_gnn_w3_b, L0_gnn_u3_w, L0_gnn_u3_b, L0_gnn_w4_w, L0_gnn_w4_b, L0_gnn_w5_w, L0_gnn_w5_b, L0_gnn_u5_w, L0_gnn_u5_b):
    import jax
    import jax.numpy as jnp

    def _L0_gnn_ref(x, in_mat, out_mat, w3_w, w3_b, u3_w, u3_b, w4_w, w4_b, w5_w, w5_b, u5_w, u5_b):
        import jax, jax.numpy as jnp
        import numpy as np
        B, N, D, T = (64, 128, 256, 3)

        def _lin(v, W, b):
            return jnp.einsum('...i,oi->...o', v, W) + b
        h = x
        for _ in range(T):
            a_in = jnp.einsum('nm,bmd->bnd', in_mat, h)
            a_out = jnp.einsum('nm,bmd->bnd', out_mat, h)
            av = jnp.concatenate([a_in, a_out], axis=-1)
            z = jax.nn.sigmoid(_lin(av, w3_w, w3_b) + _lin(h, u3_w, u3_b))
            r = jax.nn.sigmoid(_lin(av, w4_w, w4_b) + _lin(h, u3_w, u3_b))
            hv = jnp.tanh(_lin(av, w5_w, w5_b) + _lin(r * h, u5_w, u5_b))
            h = (1.0 - z) * h + z * hv
        return h
    x = _layernorm(x + _L0_gnn_ref(x, adj, adj, L0_gnn_w3_w, L0_gnn_w3_b, L0_gnn_u3_w, L0_gnn_u3_b, L0_gnn_w4_w, L0_gnn_w4_b, L0_gnn_w5_w, L0_gnn_w5_b, L0_gnn_u5_w, L0_gnn_u5_b), axis=-1)
    return x

_drawn_inputs = setup_inputs


def setup_inputs(seed=0):
    import zlib

    import numpy as np

    out = dict(_drawn_inputs(seed))
    spreads = {'L0_gnn_w3_b': (0.0, 0.442),
     'L0_gnn_u3_b': (0.0, 0.387),
     'L0_gnn_w4_b': (0.0, 0.8),
     'L0_gnn_w5_b': (0.0, 0.1),
     'L0_gnn_u5_b': (0.0, 0.1)}
    factors = {'L0_gnn_w4_w': 3.296}
    for name, (base, spread) in spreads.items():
        noise = np.random.default_rng([zlib.crc32(name.encode()), seed]).standard_normal(out[name].shape)
        drawn = base * np.exp(spread * noise) if base else spread * noise
        out[name] = jnp.asarray(drawn.astype(out[name].dtype))
    for name, factor in factors.items():
        out[name] = (out[name] * factor).astype(out[name].dtype)
    return out
```

```python
from contextlib import ExitStack

import concourse.bass as bass
from concourse import mybir

F32 = mybir.dt.float32
F32R = mybir.dt.float32r
ALU = mybir.AluOpType
ACT = mybir.ActivationFunctionType

STEPS = 3
SLOTS = 2
P = 128
EPS = 1e-5


def build(nc, x, adj, w3_w, w3_b, u3_w, u3_b, w4_w, w4_b, w5_w, w5_b, u5_w, u5_b, out):
    B, N, D = x.shape
    ROWS = 512
    GB = ROWS // N
    C = D // P
    HB = GB // 2
    HALF = ROWS // 2
    FR = STEPS * SLOTS
    PAIRS = B // (GB * SLOTS)
    DMA = 16
    assert N == P and C == 2 and GB == 4 and PAIRS * GB * SLOTS == B

    x_rows = x.rearrange("b n d -> n b d")
    out_rows = out.rearrange("b n d -> n b d")

    ctx = ExitStack()
    with ctx:
        def sb(name, shape, dt=F32):
            return ctx.enter_context(nc.sbuf_tensor(name, shape, dt))

        def ps(name):
            return ctx.enter_context(nc.psum_tensor(name, [P, 2, ROWS], F32))

        def sem(name):
            return ctx.enter_context(nc.semaphore(name))

        ident = sb("ident", [P, P])
        neg_half = sb("neg_half", [P, GB])
        wide = [sb(f"wide{k}", [P, C, 2 * D]) for k in range(3)]
        square = [sb(f"square{k}", [P, C, D]) for k in range(2)]
        wsum = [sb(f"wsum{k}", [P, C, D]) for k in range(3)]
        adj_in = sb("adj_in", [P, N])
        bias_rows = sb("bias_rows", [5 * C, P])
        bias_in = sb("bias_in", [P, 5, C])
        bias = sb("bias", [P, 3, C])
        wt_hi = [sb(f"wt_hi{k}", [P, C, D], F32R) for k in range(5)]
        wt_lo = [sb(f"wt_lo{k}", [P, C, D], F32R) for k in range(5)]
        adjT_hi = sb("adjT_hi", [P, N], F32R)
        adjT_lo = sb("adjT_lo", [P, N], F32R)
        W3, W4, W5, U3, U5 = range(5)
        BZ, BR, BV = range(3)

        x_in = [sb(f"x_in{q}", [P, GB, D]) for q in range(SLOTS)]
        x_res = [sb(f"x_res{q}", [P, GB, D]) for q in range(SLOTS)]
        y = [sb(f"y{q}", [P, GB, D]) for q in range(SLOTS)]
        hT = [sb(f"hT{q}", [P, C, ROWS]) for q in range(SLOTS)]
        z = [sb(f"z{q}", [P, C, ROWS]) for q in range(SLOTS)]
        stats = [sb(f"stats{q}", [P, GB, 6]) for q in range(SLOTS)]
        meanvar = [sb(f"meanvar{q}", [P, GB, 2]) for q in range(SLOTS)]
        var_eps = [sb(f"var_eps{q}", [P, GB]) for q in range(SLOTS)]
        rstd = [sb(f"rstd{q}", [P, GB]) for q in range(SLOTS)]

        hT_hi = sb("hT_hi", [P, C, ROWS], F32R)
        hT_lo = sb("hT_lo", [P, C, ROWS], F32R)
        hn_hi = sb("hn_hi", [P, GB, D], F32R)
        hn_lo = sb("hn_lo", [P, GB, D], F32R)
        aT_hi = sb("aT_hi", [P, C, ROWS], F32R)
        aT_lo = sb("aT_lo", [P, C, ROWS], F32R)
        u_sb = sb("u_sb", [P, C, ROWS])
        rh = sb("rh", [P, C, ROWS])
        rh_hi = sb("rh_hi", [P, C, ROWS], F32R)
        rh_lo = sb("rh_lo", [P, C, ROWS], F32R)
        dz = sb("dz", [P, C, ROWS])

        ps_v, ps_uz, ps_a, ps_tr = ps("ps_v"), ps("ps_uz"), ps("ps_a"), ps("ps_tr")

        def f32(t):
            return t.bitcast(F32)

        def half(t, h):
            return t[:, :, h * HALF:(h + 1) * HALF]

        def by_chunk(bank):
            return bank.rearrange("p (c r) -> p c r", c=C)

        def by_batch(bank):
            return bank.rearrange("p (b d) -> p b d", b=HB)

        w_loaded = [sem(f"w_loaded{k}") for k in range(5)]
        adj_loaded, bias_loaded = sem("adj_loaded"), sem("bias_loaded")
        ident_zero, ident_ready, neg_half_ready = sem("ident_zero"), sem("ident_ready"), sem("neg_half_ready")
        wsum_ready, bias_ready = sem("wsum_ready"), sem("bias_ready")
        bias_transposed, bias_copied = sem("bias_transposed"), sem("bias_copied")
        wt_transposed, wt_hi_ready, wt_lo_ready = sem("wt_transposed"), sem("wt_hi_ready"), sem("wt_lo_ready")

        x_loaded = [sem(f"x_loaded{q}") for q in range(SLOTS)]
        stored = [sem(f"stored{q}") for q in range(SLOTS)]
        x_transposed = [sem(f"x_transposed{q}") for q in range(SLOTS)]
        x_split = [sem(f"x_split{q}") for q in range(SLOTS)]
        h0_lo_ready = [sem(f"h0_lo_ready{q}") for q in range(SLOTS)]
        h0_ready = [sem(f"h0_ready{q}") for q in range(SLOTS)]
        x_kept = [sem(f"x_kept{q}") for q in range(SLOTS)]
        h_out = [sem(f"h_out{q}") for q in range(SLOTS)]
        y_ready = [sem(f"y_ready{q}") for q in range(SLOTS)]
        stats_ready = [sem(f"stats_ready{q}") for q in range(SLOTS)]
        meanvar_ready = [sem(f"meanvar_ready{q}") for q in range(SLOTS)]
        var_eps_ready = [sem(f"var_eps_ready{q}") for q in range(SLOTS)]
        rstd_ready = [sem(f"rstd_ready{q}") for q in range(SLOTS)]
        normed = [sem(f"normed{q}") for q in range(SLOTS)]

        hT_hi_ready = sem("hT_hi_ready")
        a_ready = sem("a_ready")
        a_hi_ready = sem("a_hi_ready")
        a_lo_ready = sem("a_lo_ready")
        u_ready = sem("u_ready")
        u_copied = sem("u_copied")
        rpre_ready = sem("rpre_ready")
        rsum_ready = sem("rsum_ready")
        r_ready = sem("r_ready")
        zpre_ready = sem("zpre_ready")
        z_ready = sem("z_ready")
        rh_ready = sem("rh_ready")
        rh_hi_ready = sem("rh_hi_ready")
        rh_lo_ready = sem("rh_lo_ready")
        vpre_ready = sem("vpre_ready")
        v_ready = sem("v_ready")
        d_ready = sem("d_ready")
        zd_ready = sem("zd_ready")
        h_ready = sem("h_ready")

        h_transposed = sem("h_transposed")
        hn_hi_ready = sem("hn_hi_ready")
        hn_lo_ready = sem("hn_lo_ready")
        hT_lo_ready = sem("hT_lo_ready")
        LATER = FR - SLOTS

        pool_passed, dve_passed = sem("pool_passed"), sem("dve_passed")

        def frames(i, j):
            return FR * i + (j + 1)

        def later(i, j):
            return LATER * i + (j + 1 - SLOTS)

        block = ctx.enter_context(nc.Block())

        @block.sync
        def _(sp):
            wide_in = [w3_w, w4_w, w5_w]
            square_in = [u3_w, u5_w]
            sp.dma_start(adj_in[:, :], adj).then_inc(adj_loaded, DMA)
            sp.dma_start(x_in[0][:, :, :], x_rows[:, 0:GB, :]).then_inc(x_loaded[0], DMA)
            for k in (W4, W3, W5):
                sp.dma_start(wide[k][:, :, :],
                             wide_in[k].rearrange("(c p) i -> p c i", p=P)).then_inc(w_loaded[k], DMA)
            sp.dma_start(x_in[1][:, :, :], x_rows[:, GB:2 * GB, :]).then_inc(x_loaded[1], DMA)

            def store(i, q):
                sp.wait_ge(normed[q], GB * (i + 1))
                sp.dma_start(out_rows[:, bass.ds((SLOTS * i + q) * GB, GB), :],
                             y[q][:, :, :]).then_inc(stored[q], DMA)

            def load(i, q):
                sp.wait_ge(x_transposed[q], C * i)
                sp.wait_ge(x_kept[q], i)
                sp.dma_start(x_in[q][:, :, :],
                             x_rows[:, bass.ds((SLOTS * i + q) * GB, GB), :]).then_inc(x_loaded[q], DMA)

            load(1, 0)
            load(1, 1)
            with sp.Fori(1, PAIRS - 1) as i:
                store(i - 1, 0)
                load(i + 1, 0)
                store(i - 1, 1)
                load(i + 1, 1)
            for i in (PAIRS - 2, PAIRS - 1):
                store(i, 0)
                store(i, 1)
            for q in range(SLOTS):
                sp.wait_ge(stored[q], DMA * PAIRS)

        @block.tensor
        def _(pe):
            def product(dst, lhs_hi, lhs_lo, rhs_hi, rhs_lo, first, last):
                nc.tensor.matmul(dst, lhs_lo, rhs_hi, start=first, stop=False, skip_group_check=True)
                nc.tensor.matmul(dst, lhs_hi, rhs_lo, start=False, stop=False, skip_group_check=True)
                return nc.tensor.matmul(dst, lhs_hi, rhs_hi, start=False, stop=last, skip_group_check=True)

            def dense(dst, k, oc, hi, lo, start, stop):
                for kc in range(C):
                    cols = slice(oc * P, (oc + 1) * P)
                    done = product(dst[:, oc, :], wt_hi[k][:, kc, cols], wt_lo[k][:, kc, cols],
                                   hi[:, kc, :], lo[:, kc, :], start and kc == 0, stop and kc == C - 1)
                return done

            def transpose_x(i, j, carry):
                q = j % SLOTS
                pe.wait_ge(x_loaded[q], DMA * (i + 1))
                if carry or j > 0:
                    pe.wait_ge(z_ready, C * frames(i, j - 1))
                for c in range(C):
                    for b in range(GB):
                        done = nc.tensor.transpose(ps_uz[:, c, b * N:(b + 1) * N],
                                                   x_in[q][:, b, c * P:(c + 1) * P], ident[:, :])
                    done.then_inc(x_transposed[q], 1)

            def transpose_h(q, signal):
                for b in range(GB):
                    bank = by_batch(ps_tr[:, b // HB, :])
                    for c in range(C):
                        done = nc.tensor.transpose(bank[:, b % HB, c * P:(c + 1) * P],
                                                   hT[q][:, c, b * N:(b + 1) * N], ident[:, :])
                    if b % HB == HB - 1:
                        done.then_inc(signal, 1)

            def last_h(i, q, before):
                pe.wait_ge(h_ready, C * frames(i, FR - SLOTS + q))
                pe.wait_ge(rh_ready, C * before)
                transpose_h(q, h_out[q])

            def aggregate(i, j, carry):
                if j < SLOTS:
                    pe.wait_ge(x_split[j], 2 * (i + 1))
                for hf in range(2):
                    if j >= SLOTS:
                        pe.wait_ge(hn_hi_ready, 2 * later(i, j) - 1 + hf)
                        pe.wait_ge(hn_lo_ready, 2 * later(i, j) - 1 + hf)
                    bank = by_chunk(ps_a[:, hf, :])
                    for bb in range(HB):
                        b = hf * HB + bb
                        for c in range(C):
                            feats = slice(c * P, (c + 1) * P)
                            done = product(bank[:, c, bb * N:(bb + 1) * N], hn_hi[:, b, feats],
                                           hn_lo[:, b, feats], adjT_hi[:, :], adjT_lo[:, :], True, True)
                    done.then_inc(a_ready, 1)

            def u_product(i, j):
                pe.wait_ge(hT_hi_ready, C * frames(i, j))
                if j < SLOTS:
                    pe.wait_ge(h0_lo_ready[j], C * (i + 1))
                else:
                    pe.wait_ge(hT_lo_ready, C * later(i, j))
                for oc in range(C):
                    dense(ps_uz, U3, oc, hT_hi, hT_lo, True, True).then_inc(u_ready, 1)

            def first_half(i, j, carry):
                if j < SLOTS:
                    transpose_x(i, j, carry)
                    if carry:
                        last_h(i - 1, j, frames(i, j - 1))
                    aggregate(i, j, carry)
                    u_product(i, j)
                else:
                    pe.wait_ge(h_ready, C * frames(i, j - SLOTS))
                    pe.wait_ge(rh_ready, C * frames(i, j - 1))
                    transpose_h(j % SLOTS, h_transposed)
                    pe.wait_ge(z_ready, C * frames(i, j - 1))
                    u_product(i, j)
                    aggregate(i, j, carry)

            def second_half(i, j, carry):
                pe.wait_ge(a_hi_ready, 2 * frames(i, j))
                pe.wait_ge(a_lo_ready, 2 * frames(i, j))
                if j < SLOTS and carry:
                    pe.wait_ge(y_ready[j], 2 * i)
                for oc in range(C):
                    dense(ps_tr, W4, oc, aT_hi, aT_lo, True, True).then_inc(rpre_ready, 1)
                for oc in range(C):
                    pe.wait_ge(u_copied, C * frames(i, j) - 1 + oc)
                    dense(ps_uz, W3, oc, aT_hi, aT_lo, False, True).then_inc(zpre_ready, 1)
                for oc in range(C):
                    if carry or j > 0:
                        pe.wait_ge(d_ready, C * frames(i, j - 1) - 1 + oc)
                    dense(ps_v, W5, oc, aT_hi, aT_lo, True, False)

            def candidate(i, j):
                pe.wait_ge(rh_hi_ready, C * frames(i, j))
                pe.wait_ge(rh_lo_ready, C * frames(i, j))
                for oc in range(C):
                    dense(ps_v, U5, oc, rh_hi, rh_lo, False, True).then_inc(vpre_ready, 1)

            pe.wait_ge(ident_ready, 1)
            pe.wait_ge(adj_loaded, DMA)
            banks = [ps_v[:, 0, :], ps_v[:, 1, :], ps_a[:, 0, :], ps_a[:, 1, :], ps_tr[:, 0, :]]
            nc.tensor.transpose(ps_tr[:, 1, 0:N], adj_in[:, :], ident[:, :]).then_inc(wt_transposed, 1)
            summed = 0
            for k in (U3, W4, W3, W5, U5):
                if k in (U3, U5):
                    pe.wait_ge(w_loaded[k], DMA)
                    src = square[k - U3]
                else:
                    summed += 1
                    pe.wait_ge(wsum_ready, summed)
                    src = wsum[k]
                dst = banks[k].rearrange("p (c o) -> p c o", c=C)
                for kc in range(C):
                    for oc in range(C):
                        done = nc.tensor.transpose(dst[:, kc, oc * P:(oc + 1) * P],
                                                   src[:, oc, kc * P:(kc + 1) * P], ident[:, :])
                done.then_inc(wt_transposed, 1)
            pe.wait_ge(bias_loaded, 5 * DMA)
            nc.tensor.transpose(ps_uz[:, 0, 0:5 * C], bias_rows[:, :],
                                ident[0:5 * C, 0:5 * C]).then_inc(bias_transposed, 1)
            pe.wait_ge(bias_copied, 1)
            pe.wait_ge(wt_hi_ready, 6)
            pe.wait_ge(wt_lo_ready, 6)

            def pair(i, carry):
                first_half(i, 0, carry)
                if carry:
                    candidate(i - 1, FR - 1)
                for j in range(FR):
                    second_half(i, j, carry)
                    if j < FR - 1:
                        first_half(i, j + 1, carry)
                        candidate(i, j)

            pair(0, False)
            with pe.Fori(1, PAIRS) as i:
                pair(i, True)
            last = PAIRS - 1
            last_h(last, 0, frames(last, FR - 1))
            candidate(last, FR - 1)
            pe.wait_ge(y_ready[0], 2 * PAIRS)
            last_h(last, 1, frames(last, FR - 1))

        @block.scalar
        def _(act):
            def split_first_half(i, j, carry):
                q = j % SLOTS
                if j < SLOTS:
                    for c in range(C):
                        act.wait_ge(x_transposed[q], C * i + c + 1)
                        if j > 0 and c == 0:
                            act.wait_ge(h0_ready[0], i + 1)
                        nc.scalar.copy(hT_hi[:, c, :], ps_uz[:, c, :]).then_inc(hT_hi_ready, 1)
                else:
                    for hf in range(2):
                        act.wait_ge(h_transposed, 2 * later(i, j) - 1 + hf)
                        nc.scalar.copy(hn_hi[:, hf * HB:(hf + 1) * HB, :],
                                       by_batch(ps_tr[:, hf, :])).then_inc(hn_hi_ready, 1)
                    copy_u(i, j)
                for hf in range(2):
                    act.wait_ge(a_ready, 2 * frames(i, j) - 1 + hf)
                    nc.scalar.copy(half(aT_hi, hf), by_chunk(ps_a[:, hf, :])).then_inc(a_hi_ready, 1)
                if j < SLOTS:
                    copy_u(i, j)

            def copy_u(i, j):
                for oc in range(C):
                    act.wait_ge(u_ready, C * frames(i, j) - 1 + oc)
                    nc.scalar.copy(u_sb[:, oc, :], ps_uz[:, oc, :]).then_inc(u_copied, 1)

            def tanh_v(i, j):
                for oc in range(C):
                    act.wait_ge(vpre_ready, C * frames(i, j) - 1 + oc)
                    nc.scalar.activation(ps_v[:, oc, :], ps_v[:, oc, :], ACT.Tanh,
                                         bias=bias[:, BV, oc:oc + 1]).then_inc(v_ready, 1)

            def pair(i, carry):
                split_first_half(i, 0, carry)
                for j in range(FR):
                    q = j % SLOTS
                    before = carry or j > 0
                    if before:
                        tanh_v(i, j - 1)
                    for oc in range(C):
                        act.wait_ge(rsum_ready, C * frames(i, j) - 1 + oc)
                        nc.scalar.activation(ps_tr[:, oc, :], ps_tr[:, oc, :], ACT.Sigmoid,
                                             bias=bias[:, BR, oc:oc + 1]).then_inc(r_ready, 1)
                        if 0 < j < FR - 1:
                            act.wait_ge(h_ready, C * frames(i, j - 1) - 1 + oc)
                            if j == 1 and oc == 0:
                                act.wait_ge(h0_ready[1], i + 1)
                            nc.scalar.copy(hT_hi[:, oc, :], hT[1 - q][:, oc, :]).then_inc(hT_hi_ready, 1)
                    for oc in range(C):
                        act.wait_ge(zpre_ready, C * frames(i, j) - 1 + oc)
                        if (carry or j >= SLOTS) and oc == 0:
                            act.wait_ge(zd_ready, C * frames(i, j - SLOTS))
                        nc.scalar.activation(z[q][:, oc, :], ps_uz[:, oc, :], ACT.Sigmoid,
                                             bias=bias[:, BZ, oc:oc + 1]).then_inc(z_ready, 1)
                        act.wait_ge(rh_ready, C * frames(i, j) - 1 + oc)
                        nc.scalar.copy(rh_hi[:, oc, :], rh[:, oc, :]).then_inc(rh_hi_ready, 1)
                    if j < FR - 1:
                        split_first_half(i, j + 1, carry)

            act.dma_start(square[0][:, :, :], u3_w.rearrange("(c p) i -> p c i", p=P)).then_inc(w_loaded[U3], DMA)
            act.dma_start(square[1][:, :, :], u5_w.rearrange("(c p) i -> p c i", p=P)).then_inc(w_loaded[U5], DMA)
            for n, b in enumerate((w3_b, u3_b, w4_b, w5_b, u5_b)):
                act.dma_start(bias_rows[C * n:C * (n + 1), :], b.rearrange("(c p) -> c p", p=P)).then_inc(bias_loaded, DMA)
            act.wait_ge(wt_transposed, 1)
            nc.scalar.copy(adjT_hi[:, :], ps_tr[:, 1, 0:N]).then_inc(wt_hi_ready, 1)
            banks = [ps_v[:, 0, :], ps_v[:, 1, :], ps_a[:, 0, :], ps_a[:, 1, :], ps_tr[:, 0, :]]
            for n, k in enumerate((U3, W4, W3, W5, U5)):
                act.wait_ge(wt_transposed, n + 2)
                nc.scalar.copy(wt_hi[k][:, :, :], banks[k].rearrange("p (c o) -> p c o", c=C)).then_inc(wt_hi_ready, 1)
            act.wait_ge(bias_transposed, 1)
            nc.scalar.copy(bias_in[:, :, :],
                           ps_uz[:, 0, 0:5 * C].rearrange("p (n c) -> p n c", c=C)).then_inc(bias_copied, 1)
            act.wait_ge(bias_ready, 3)

            pair(0, False)
            with act.Fori(1, PAIRS) as i:
                pair(i, True)
            tanh_v(PAIRS - 1, FR - 1)

        @block.vector
        def _(dve):
            def residual(i, q, carry):
                dve.wait_ge(x_kept[q], i + 1)
                if carry:
                    dve.wait_ge(stored[q], DMA * i)
                for hf in range(2):
                    dve.wait_ge(h_out[q], 2 * i + hf + 1)
                    part = slice(hf * HB, (hf + 1) * HB)
                    nc.vector.tensor_tensor(y[q][:, part, :], by_batch(ps_tr[:, hf, :]), x_res[q][:, part, :],
                                            ALU.add).then_inc(y_ready[q], 1)

            def statistics(i, q):
                dve.wait_ge(y_ready[q], 2 * (i + 1))
                for b in range(GB):
                    nc.vector.bn_stats(stats[q][:, b, :], y[q][:, b, :]).then_inc(stats_ready[q], 1)
                dve.wait_ge(stats_ready[q], GB * (i + 1))
                dve.sem_inc(dve_passed, 1)
                for b in range(GB):
                    nc.vector.bn_aggr(meanvar[q][:, b, :], stats[q][:, b, :]).then_inc(meanvar_ready[q], 1)

            def split_first_half(i, j, carry, out_carry):
                q = j % SLOTS
                if j < SLOTS:
                    for c in range(C):
                        if j > 0 and c == 0:
                            dve.wait_ge(h0_ready[0], i + 1)
                        dve.wait_ge(hT_hi_ready, C * frames(i, j) - 1 + c)
                        nc.vector.tensor_tensor(hT_lo[:, c, :], ps_uz[:, c, :], f32(hT_hi[:, c, :]),
                                                ALU.subtract).then_inc(h0_lo_ready[q], 1)
                    if carry:
                        residual(i - 1, q, out_carry)
                else:
                    for hf in range(2):
                        dve.wait_ge(hn_hi_ready, 2 * later(i, j) - 1 + hf)
                        part = slice(hf * HB, (hf + 1) * HB)
                        nc.vector.tensor_tensor(hn_lo[:, part, :], by_batch(ps_tr[:, hf, :]),
                                                f32(hn_hi[:, part, :]), ALU.subtract).then_inc(hn_lo_ready, 1)
                for hf in range(2):
                    dve.wait_ge(a_hi_ready, 2 * frames(i, j) - 1 + hf)
                    nc.vector.tensor_tensor(half(aT_lo, hf), by_chunk(ps_a[:, hf, :]), f32(half(aT_hi, hf)),
                                            ALU.subtract).then_inc(a_lo_ready, 1)

            def v_minus_h(i, j, c):
                dve.wait_ge(v_ready, C * frames(i, j) - 1 + c)
                nc.vector.tensor_tensor(dz[:, c, :], ps_v[:, c, :], hT[j % SLOTS][:, c, :],
                                        ALU.subtract).then_inc(d_ready, 1)

            def times_z(i, j, c):
                dve.wait_ge(d_ready, C * frames(i, j) - 1 + c)
                nc.vector.tensor_tensor(dz[:, c, :], dz[:, c, :], z[j % SLOTS][:, c, :],
                                        ALU.mult).then_inc(zd_ready, 1)

            def new_h(i, j, c):
                dve.wait_ge(zd_ready, C * frames(i, j) - 1 + c)
                nc.vector.tensor_tensor(hT[j % SLOTS][:, c, :], dz[:, c, :], hT[j % SLOTS][:, c, :],
                                        ALU.add).then_inc(h_ready, 1)

            def add_u(i, j, c):
                dve.wait_ge(rpre_ready, C * frames(i, j) - 1 + c)
                dve.wait_ge(u_copied, C * frames(i, j) - 1 + c)
                nc.vector.tensor_tensor(ps_tr[:, c, :], ps_tr[:, c, :], u_sb[:, c, :],
                                        ALU.add).then_inc(rsum_ready, 1)

            def times_r(i, j, c):
                dve.wait_ge(r_ready, C * frames(i, j) - 1 + c)
                if j < SLOTS:
                    dve.wait_ge(h0_ready[j], i + 1)
                nc.vector.tensor_tensor(rh[:, c, :], ps_tr[:, c, :], hT[j % SLOTS][:, c, :],
                                        ALU.mult).then_inc(rh_ready, 1)

            def rh_low(i, j, c):
                dve.wait_ge(rh_hi_ready, C * frames(i, j) - 1 + c)
                nc.vector.tensor_tensor(rh_lo[:, c, :], rh[:, c, :], f32(rh_hi[:, c, :]),
                                        ALU.subtract).then_inc(rh_lo_ready, 1)

            def pair(i, carry, out_carry):
                split_first_half(i, 0, carry, out_carry)
                for j in range(FR):
                    before = carry or j > 0
                    if before:
                        v_minus_h(i, j - 1, 0)
                        times_z(i, j - 1, 0)
                        v_minus_h(i, j - 1, 1)
                        new_h(i, j - 1, 0)
                        times_z(i, j - 1, 1)
                    add_u(i, j, 0)
                    if before:
                        new_h(i, j - 1, 1)
                    times_r(i, j, 0)
                    add_u(i, j, 1)
                    times_r(i, j, 1)
                    rh_low(i, j, 0)
                    rh_low(i, j, 1)
                    if j < SLOTS and carry:
                        statistics(i - 1, j)
                    if j < FR - 1:
                        split_first_half(i, j + 1, carry, out_carry)

            for k in (W4, W3, W5):
                dve.wait_ge(w_loaded[k], DMA)
                nc.vector.tensor_tensor(wsum[k][:, :, :], wide[k][:, :, 0:D], wide[k][:, :, D:2 * D],
                                        ALU.add).then_inc(wsum_ready, 1)
            dve.wait_ge(wt_hi_ready, 1)
            nc.vector.tensor_tensor(adjT_lo[:, :], ps_tr[:, 1, 0:N], f32(adjT_hi[:, :]),
                                    ALU.subtract).then_inc(wt_lo_ready, 1)
            banks = [ps_v[:, 0, :], ps_v[:, 1, :], ps_a[:, 0, :], ps_a[:, 1, :], ps_tr[:, 0, :]]
            for n, k in enumerate((U3, W4, W3, W5, U5)):
                dve.wait_ge(wt_hi_ready, n + 2)
                nc.vector.tensor_tensor(wt_lo[k][:, :, :], banks[k].rearrange("p (c o) -> p c o", c=C),
                                        f32(wt_hi[k][:, :, :]), ALU.subtract).then_inc(wt_lo_ready, 1)
            dve.wait_ge(bias_copied, 1)
            for b, (l, r) in ((BZ, (0, 1)), (BR, (2, 1)), (BV, (3, 4))):
                nc.vector.tensor_tensor(bias[:, b, :], bias_in[:, l, :], bias_in[:, r, :],
                                        ALU.add).then_inc(bias_ready, 1)

            pair(0, False, False)
            with dve.Fori(1, PAIRS) as i:
                pair(i, True, True)
            last = PAIRS - 1
            residual(last, 0, True)
            for c in range(C):
                v_minus_h(last, FR - 1, c)
                times_z(last, FR - 1, c)
                new_h(last, FR - 1, c)
            statistics(last, 0)
            residual(last, 1, True)
            statistics(last, 1)

        @block.gpsimd
        def _(pool):
            def split_x(i, j, carry):
                q = j
                pool.wait_ge(x_loaded[q], DMA * (i + 1))
                if carry or j > 0:
                    pool.wait_ge(a_ready, 2 * frames(i, j - 1))
                pool.sem_inc(pool_passed, 1)
                nc.gpsimd.tensor_copy(hn_hi[:, :, :], x_in[q][:, :, :]).then_inc(x_split[q], 1)
                pool.wait_ge(x_split[q], 2 * i + 1)
                nc.gpsimd.tensor_tensor(hn_lo[:, :, :], x_in[q][:, :, :], f32(hn_hi[:, :, :]),
                                        ALU.subtract).then_inc(x_split[q], 1)

            def first_h(i, j, carry):
                q = j
                pool.wait_ge(hT_hi_ready, C * frames(i, j))
                pool.wait_ge(h0_lo_ready[q], C * (i + 1))
                if carry:
                    pool.wait_ge(h_out[q], 2 * i)
                nc.gpsimd.tensor_tensor(hT[q][:, :, :], f32(hT_hi[:, :, :]), f32(hT_lo[:, :, :]),
                                        ALU.add).then_inc(h0_ready[q], 1)

            def keep_x(i, q, carry):
                if carry:
                    pool.wait_ge(y_ready[q], 2 * i)
                    pool.sem_inc(pool_passed, 1)
                nc.gpsimd.tensor_copy(x_res[q][:, :, :], x_in[q][:, :, :]).then_inc(x_kept[q], 1)

            def normalise(i, q):
                pool.wait_ge(meanvar_ready[q], GB * (i + 1))
                pool.sem_inc(pool_passed, 1)
                nc.gpsimd.tensor_scalar(var_eps[q][:, :], meanvar[q][:, :, 1], EPS, None,
                                        ALU.add).then_inc(var_eps_ready[q], 1)
                pool.wait_ge(var_eps_ready[q], i + 1)
                nc.gpsimd.tensor_tensor(rstd[q][:, :], var_eps[q][:, :], neg_half[:, :],
                                        ALU.pow).then_inc(rstd_ready[q], 1)
                pool.wait_ge(rstd_ready[q], i + 1)
                pool.sem_inc(pool_passed, 1)
                for b in range(GB):
                    nc.gpsimd.tensor_scalar(y[q][:, b, :], y[q][:, b, :], meanvar[q][:, b, 0:1],
                                            rstd[q][:, b:b + 1], ALU.subtract, ALU.mult).then_inc(normed[q], 1)

            def pair(i, carry):
                split_x(i, 0, carry)
                first_h(i, 0, carry)
                keep_x(i, 0, carry)
                split_x(i, 1, carry)
                if carry:
                    normalise(i - 1, 0)
                first_h(i, 1, carry)
                keep_x(i, 1, carry)
                for j in range(SLOTS, FR):
                    for c in range(C):
                        pool.wait_ge(h_ready, C * frames(i, j - SLOTS) - 1 + c)
                        pool.wait_ge(hT_hi_ready, C * frames(i, j) - 1 + c)
                        nc.gpsimd.tensor_tensor(hT_lo[:, c, :], hT[j % SLOTS][:, c, :], f32(hT_hi[:, c, :]),
                                                ALU.subtract).then_inc(hT_lo_ready, 1)
                    if j == SLOTS and carry:
                        normalise(i - 1, 1)

            nc.gpsimd.memset(ident[:, :], 0.0).then_inc(ident_zero, 1)
            pool.wait_ge(ident_zero, 1)
            nc.gpsimd.affine_select(out=ident[:, :], in_=ident[:, :], compare_op=ALU.not_equal, fill=1.0,
                                    base=0, pattern=[[-1, P]], channel_multiplier=1).then_inc(ident_ready, 1)
            nc.gpsimd.memset(neg_half[:, :], -0.5).then_inc(neg_half_ready, 1)
            pool.wait_ge(neg_half_ready, 1)

            pair(0, False)
            with pool.Fori(1, PAIRS) as i:
                pair(i, True)
            normalise(PAIRS - 1, 0)
            normalise(PAIRS - 1, 1)


_INS = ["x", "adj", "L0_gnn_w3_w", "L0_gnn_w3_b", "L0_gnn_u3_w", "L0_gnn_u3_b", "L0_gnn_w4_w", "L0_gnn_w4_b",
        "L0_gnn_w5_w", "L0_gnn_w5_b", "L0_gnn_u5_w", "L0_gnn_u5_b"]


def kernel(**inputs):
    import numpy as np
    import concourse.bacc as bacc
    from concourse.bass_utils import run_bass_kernel_spmd

    nc = bacc.Bacc("TRN2", target_bir_lowering=False, num_devices=1)
    arrays, args = {}, []
    for name in _INS:
        a = np.ascontiguousarray(inputs[name])
        arrays[f"in_{name}"] = a
        args.append(nc.dram_tensor(f"in_{name}", a.shape, mybir.dt.from_np(a.dtype), kind="ExternalInput").ap())
    args.append(nc.dram_tensor("out", inputs["x"].shape, F32, kind="ExternalOutput").ap())
    build(nc, *args)
    result = run_bass_kernel_spmd(nc, [arrays], core_ids=[0])
    return result.results[0]["out"]
```

```python
from contextlib import ExitStack

import concourse.bass as bass
from concourse import mybir

F32 = mybir.dt.float32
F32R = mybir.dt.float32r
ALU = mybir.AluOpType
ACT = mybir.ActivationFunctionType

STEPS = 3
SLOTS = 2
P = 128
EPS = 1e-5


def build(nc, x, adj, w3_w, w3_b, u3_w, u3_b, w4_w, w4_b, w5_w, w5_b, u5_w, u5_b, out):
    B, N, D = x.shape
    ROWS = 512
    GB = ROWS // N
    C = D // P
    HB = GB // 2
    HALF = ROWS // 2
    FR = STEPS * SLOTS
    PAIRS = B // (GB * SLOTS)
    DMA = 16
    assert N == P and C == 2 and GB == 4 and PAIRS * GB * SLOTS == B

    x_rows = x.rearrange("b n d -> n b d")
    out_rows = out.rearrange("b n d -> n b d")

    ctx = ExitStack()
    with ctx:
        def sb(name, shape, dt=F32):
            return ctx.enter_context(nc.sbuf_tensor(name, shape, dt))

        def ps(name):
            return ctx.enter_context(nc.psum_tensor(name, [P, 2, ROWS], F32))

        def sem(name):
            return ctx.enter_context(nc.semaphore(name))

        ident = sb("ident", [P, P])
        neg_half = sb("neg_half", [P, GB])
        wide = [sb(f"wide{k}", [P, C, 2 * D]) for k in range(3)]
        square = [sb(f"square{k}", [P, C, D]) for k in range(2)]
        wsum = [sb(f"wsum{k}", [P, C, D]) for k in range(3)]
        adj_in = sb("adj_in", [P, N])
        bias_rows = sb("bias_rows", [5 * C, P])
        bias_in = sb("bias_in", [P, 5, C])
        bias = sb("bias", [P, 3, C])
        wt_hi = [sb(f"wt_hi{k}", [P, C, D], F32R) for k in range(5)]
        wt_lo = [sb(f"wt_lo{k}", [P, C, D], F32R) for k in range(5)]
        adjT = sb("adjT", [P, N])
        W3, W4, W5, U3, U5 = range(5)
        BZ, BR, BV = range(3)

        x_in = [sb(f"x_in{q}", [P, GB, D]) for q in range(SLOTS)]
        x_res = [sb(f"x_res{q}", [P, GB, D]) for q in range(SLOTS)]
        y = [sb(f"y{q}", [P, GB, D]) for q in range(SLOTS)]
        hT = [sb(f"hT{q}", [P, C, ROWS]) for q in range(SLOTS)]
        z = [sb(f"z{q}", [P, C, ROWS]) for q in range(SLOTS)]
        stats = [sb(f"stats{q}", [P, GB, 6]) for q in range(SLOTS)]
        meanvar = [sb(f"meanvar{q}", [P, GB, 2]) for q in range(SLOTS)]
        var_eps = [sb(f"var_eps{q}", [P, GB]) for q in range(SLOTS)]
        neg_mean = [sb(f"neg_mean{q}", [P, GB]) for q in range(SLOTS)]
        rstd = [sb(f"rstd{q}", [P, GB]) for q in range(SLOTS)]
        shift = [sb(f"shift{q}", [P, GB]) for q in range(SLOTS)]

        hT_hi = sb("hT_hi", [P, C, ROWS], F32R)
        hT_lo = sb("hT_lo", [P, C, ROWS], F32R)
        hn = sb("hn", [P, GB, D])
        aT_hi = sb("aT_hi", [P, C, ROWS], F32R)
        aT_lo = sb("aT_lo", [P, C, ROWS], F32R)
        u_sb = sb("u_sb", [P, C, ROWS])
        rh = sb("rh", [P, C, ROWS])
        rh_hi = sb("rh_hi", [P, C, ROWS], F32R)
        rh_lo = sb("rh_lo", [P, C, ROWS], F32R)
        dz = sb("dz", [P, C, ROWS])

        ps_v, ps_uz, ps_a, ps_tr = ps("ps_v"), ps("ps_uz"), ps("ps_a"), ps("ps_tr")

        def f32(t):
            return t.bitcast(F32)

        def half(t, h):
            return t[:, :, h * HALF:(h + 1) * HALF]

        def by_chunk(bank):
            return bank.rearrange("p (c r) -> p c r", c=C)

        def by_batch(bank):
            return bank.rearrange("p (b d) -> p b d", b=HB)

        w_loaded = [sem(f"w_loaded{k}") for k in range(5)]
        adj_loaded, bias_loaded = sem("adj_loaded"), sem("bias_loaded")
        ident_zero, ident_ready, neg_half_ready = sem("ident_zero"), sem("ident_ready"), sem("neg_half_ready")
        wsum_ready, bias_ready = sem("wsum_ready"), sem("bias_ready")
        bias_transposed, bias_copied = sem("bias_transposed"), sem("bias_copied")
        wt_transposed, wt_hi_ready, wt_lo_ready = sem("wt_transposed"), sem("wt_hi_ready"), sem("wt_lo_ready")

        x_loaded = [sem(f"x_loaded{q}") for q in range(SLOTS)]
        stored = [sem(f"stored{q}") for q in range(SLOTS)]
        x_transposed = [sem(f"x_transposed{q}") for q in range(SLOTS)]
        h0_lo_ready = [sem(f"h0_lo_ready{q}") for q in range(SLOTS)]
        h0_ready = [sem(f"h0_ready{q}") for q in range(SLOTS)]
        x_kept = [sem(f"x_kept{q}") for q in range(SLOTS)]
        h_out = [sem(f"h_out{q}") for q in range(SLOTS)]
        y_ready = [sem(f"y_ready{q}") for q in range(SLOTS)]
        stats_ready = [sem(f"stats_ready{q}") for q in range(SLOTS)]
        meanvar_ready = [sem(f"meanvar_ready{q}") for q in range(SLOTS)]
        var_eps_ready = [sem(f"var_eps_ready{q}") for q in range(SLOTS)]
        neg_mean_ready = [sem(f"neg_mean_ready{q}") for q in range(SLOTS)]
        rstd_ready = [sem(f"rstd_ready{q}") for q in range(SLOTS)]
        shift_ready = [sem(f"shift_ready{q}") for q in range(SLOTS)]
        normed = [sem(f"normed{q}") for q in range(SLOTS)]

        hT_hi_ready = sem("hT_hi_ready")
        a_ready = sem("a_ready")
        a_hi_ready = sem("a_hi_ready")
        a_lo_ready = sem("a_lo_ready")
        u_ready = sem("u_ready")
        u_copied = sem("u_copied")
        rpre_ready = sem("rpre_ready")
        rsum_ready = sem("rsum_ready")
        r_ready = sem("r_ready")
        zpre_ready = sem("zpre_ready")
        z_ready = sem("z_ready")
        rh_ready = sem("rh_ready")
        rh_hi_ready = sem("rh_hi_ready")
        rh_lo_ready = sem("rh_lo_ready")
        vpre_ready = sem("vpre_ready")
        v_ready = sem("v_ready")
        d_ready = sem("d_ready")
        zd_ready = sem("zd_ready")
        h_ready = sem("h_ready")

        h_transposed = sem("h_transposed")
        hn_ready = sem("hn_ready")
        hT_lo_ready = sem("hT_lo_ready")
        LATER = FR - SLOTS

        pool_passed, dve_passed = sem("pool_passed"), sem("dve_passed")

        def frames(i, j):
            return FR * i + (j + 1)

        def later(i, j):
            return LATER * i + (j + 1 - SLOTS)

        block = ctx.enter_context(nc.Block())

        @block.sync
        def _(sp):
            wide_in = [w3_w, w4_w, w5_w]
            square_in = [u3_w, u5_w]
            sp.dma_start(adj_in[:, :], adj).then_inc(adj_loaded, DMA)
            sp.dma_start(x_in[0][:, :, :], x_rows[:, 0:GB, :]).then_inc(x_loaded[0], DMA)
            for k in (W4, W3, W5):
                sp.dma_start(wide[k][:, :, :],
                             wide_in[k].rearrange("(c p) i -> p c i", p=P)).then_inc(w_loaded[k], DMA)
            sp.dma_start(x_in[1][:, :, :], x_rows[:, GB:2 * GB, :]).then_inc(x_loaded[1], DMA)

            def store(i, q):
                sp.wait_ge(normed[q], GB * (i + 1))
                sp.dma_start(out_rows[:, bass.ds((SLOTS * i + q) * GB, GB), :],
                             y[q][:, :, :]).then_inc(stored[q], DMA)

            def load(i, q):
                sp.wait_ge(x_kept[q], i)
                sp.wait_ge(a_ready, 2 * frames(i - 1, q))
                sp.dma_start(x_in[q][:, :, :],
                             x_rows[:, bass.ds((SLOTS * i + q) * GB, GB), :]).then_inc(x_loaded[q], DMA)

            load(1, 0)
            load(1, 1)
            with sp.Fori(1, PAIRS - 1) as i:
                store(i - 1, 0)
                load(i + 1, 0)
                store(i - 1, 1)
                load(i + 1, 1)
            for i in (PAIRS - 2, PAIRS - 1):
                store(i, 0)
                store(i, 1)
            for q in range(SLOTS):
                sp.wait_ge(stored[q], DMA * PAIRS)

        @block.tensor
        def _(pe):
            def product(dst, lhs_hi, lhs_lo, rhs_hi, rhs_lo, first, last):
                nc.tensor.matmul(dst, lhs_lo, rhs_hi, start=first, stop=False, skip_group_check=True)
                nc.tensor.matmul(dst, lhs_hi, rhs_lo, start=False, stop=False, skip_group_check=True)
                return nc.tensor.matmul(dst, lhs_hi, rhs_hi, start=False, stop=last, skip_group_check=True)

            def dense(dst, k, oc, hi, lo, start, stop):
                for kc in range(C):
                    cols = slice(oc * P, (oc + 1) * P)
                    done = product(dst[:, oc, :], wt_hi[k][:, kc, cols], wt_lo[k][:, kc, cols],
                                   hi[:, kc, :], lo[:, kc, :], start and kc == 0, stop and kc == C - 1)
                return done

            def transpose_x(i, j, carry):
                q = j % SLOTS
                pe.wait_ge(x_loaded[q], DMA * (i + 1))
                if carry or j > 0:
                    pe.wait_ge(z_ready, C * frames(i, j - 1))
                for c in range(C):
                    for b in range(GB):
                        done = nc.tensor.transpose(ps_uz[:, c, b * N:(b + 1) * N],
                                                   x_in[q][:, b, c * P:(c + 1) * P], ident[:, :])
                    done.then_inc(x_transposed[q], 1)

            def transpose_h(q, signal):
                for b in range(GB):
                    bank = by_batch(ps_tr[:, b // HB, :])
                    for c in range(C):
                        done = nc.tensor.transpose(bank[:, b % HB, c * P:(c + 1) * P],
                                                   hT[q][:, c, b * N:(b + 1) * N], ident[:, :])
                    if b % HB == HB - 1:
                        done.then_inc(signal, 1)

            def last_h(i, q, before):
                pe.wait_ge(h_ready, C * frames(i, FR - SLOTS + q))
                pe.wait_ge(rh_ready, C * before)
                transpose_h(q, h_out[q])

            def aggregate(i, j):
                src = x_in[j] if j < SLOTS else hn
                for hf in range(2):
                    if j >= SLOTS:
                        pe.wait_ge(hn_ready, 2 * later(i, j) - 1 + hf)
                    bank = by_chunk(ps_a[:, hf, :])
                    for bb in range(HB):
                        b = hf * HB + bb
                        for c in range(C):
                            feats = slice(c * P, (c + 1) * P)
                            done = nc.tensor.matmul(bank[:, c, bb * N:(bb + 1) * N], src[:, b, feats],
                                                    adjT[:, :], start=True, stop=True)
                    done.then_inc(a_ready, 1)

            def u_product(i, j):
                pe.wait_ge(hT_hi_ready, C * frames(i, j))
                if j < SLOTS:
                    pe.wait_ge(h0_lo_ready[j], C * (i + 1))
                    pe.wait_ge(h0_ready[j], C * (i + 1))
                else:
                    pe.wait_ge(hT_lo_ready, C * later(i, j))
                for oc in range(C):
                    dense(ps_uz, U3, oc, hT_hi, hT_lo, True, True).then_inc(u_ready, 1)

            def first_half(i, j, carry):
                if j < SLOTS:
                    transpose_x(i, j, carry)
                    if carry:
                        last_h(i - 1, j, frames(i, j - 1))
                    aggregate(i, j)
                    u_product(i, j)
                else:
                    pe.wait_ge(h_ready, C * frames(i, j - SLOTS))
                    pe.wait_ge(rh_ready, C * frames(i, j - 1))
                    transpose_h(j % SLOTS, h_transposed)
                    pe.wait_ge(z_ready, C * frames(i, j - 1))
                    u_product(i, j)
                    aggregate(i, j)

            def second_half(i, j, carry):
                pe.wait_ge(a_hi_ready, 2 * frames(i, j))
                pe.wait_ge(a_lo_ready, 2 * frames(i, j))
                if j < SLOTS and carry:
                    pe.wait_ge(y_ready[j], 2 * i)
                for oc in range(C):
                    dense(ps_tr, W4, oc, aT_hi, aT_lo, True, True).then_inc(rpre_ready, 1)
                for oc in range(C):
                    pe.wait_ge(u_copied, C * frames(i, j) - 1 + oc)
                    dense(ps_uz, W3, oc, aT_hi, aT_lo, False, True).then_inc(zpre_ready, 1)
                for oc in range(C):
                    if carry or j > 0:
                        pe.wait_ge(d_ready, C * frames(i, j - 1) - 1 + oc)
                    dense(ps_v, W5, oc, aT_hi, aT_lo, True, False)

            def candidate(i, j):
                pe.wait_ge(rh_hi_ready, C * frames(i, j))
                pe.wait_ge(rh_lo_ready, C * frames(i, j))
                for oc in range(C):
                    dense(ps_v, U5, oc, rh_hi, rh_lo, False, True).then_inc(vpre_ready, 1)

            pe.wait_ge(ident_ready, 1)
            pe.wait_ge(adj_loaded, DMA)
            banks = [ps_v[:, 0, :], ps_v[:, 1, :], ps_a[:, 0, :], ps_a[:, 1, :], ps_tr[:, 0, :]]
            nc.tensor.transpose(ps_tr[:, 1, 0:N], adj_in[:, :], ident[:, :]).then_inc(wt_transposed, 1)
            summed = 0
            for k in (U3, W4, W3, W5, U5):
                if k in (U3, U5):
                    pe.wait_ge(w_loaded[k], DMA)
                    src = square[k - U3]
                else:
                    summed += 1
                    pe.wait_ge(wsum_ready, summed)
                    src = wsum[k]
                dst = banks[k].rearrange("p (c o) -> p c o", c=C)
                for kc in range(C):
                    for oc in range(C):
                        done = nc.tensor.transpose(dst[:, kc, oc * P:(oc + 1) * P],
                                                   src[:, oc, kc * P:(kc + 1) * P], ident[:, :])
                done.then_inc(wt_transposed, 1)
            pe.wait_ge(bias_loaded, 5 * DMA)
            nc.tensor.transpose(ps_uz[:, 0, 0:5 * C], bias_rows[:, :],
                                ident[0:5 * C, 0:5 * C]).then_inc(bias_transposed, 1)
            pe.wait_ge(bias_copied, 1)
            pe.wait_ge(wt_hi_ready, 6)
            pe.wait_ge(wt_lo_ready, 5)

            def pair(i, carry):
                first_half(i, 0, carry)
                if carry:
                    candidate(i - 1, FR - 1)
                for j in range(FR):
                    second_half(i, j, carry)
                    if j < FR - 1:
                        first_half(i, j + 1, carry)
                        candidate(i, j)

            pair(0, False)
            with pe.Fori(1, PAIRS) as i:
                pair(i, True)
            last = PAIRS - 1
            last_h(last, 0, frames(last, FR - 1))
            candidate(last, FR - 1)
            pe.wait_ge(y_ready[0], 2 * PAIRS)
            last_h(last, 1, frames(last, FR - 1))

        @block.scalar
        def _(act):
            def split_first_half(i, j, carry):
                q = j % SLOTS
                if j < SLOTS:
                    for c in range(C):
                        act.wait_ge(x_transposed[q], C * i + c + 1)
                        nc.scalar.copy(hT_hi[:, c, :], ps_uz[:, c, :]).then_inc(hT_hi_ready, 1)
                    if carry:
                        act.wait_ge(h_out[q], 2 * i)
                    for c in range(C):
                        act.wait_ge(h0_lo_ready[q], C * i + c + 1)
                        nc.scalar.copy(hT[q][:, c, :], ps_uz[:, c, :]).then_inc(h0_ready[q], 1)
                else:
                    for hf in range(2):
                        act.wait_ge(h_transposed, 2 * later(i, j) - 1 + hf)
                        nc.scalar.copy(hn[:, hf * HB:(hf + 1) * HB, :],
                                       by_batch(ps_tr[:, hf, :])).then_inc(hn_ready, 1)
                    copy_u(i, j)
                for hf in range(2):
                    act.wait_ge(a_ready, 2 * frames(i, j) - 1 + hf)
                    nc.scalar.copy(half(aT_hi, hf), by_chunk(ps_a[:, hf, :])).then_inc(a_hi_ready, 1)
                if j < SLOTS:
                    copy_u(i, j)

            def copy_u(i, j):
                for oc in range(C):
                    act.wait_ge(u_ready, C * frames(i, j) - 1 + oc)
                    nc.scalar.copy(u_sb[:, oc, :], ps_uz[:, oc, :]).then_inc(u_copied, 1)

            def tanh_v(i, j):
                for oc in range(C):
                    act.wait_ge(vpre_ready, C * frames(i, j) - 1 + oc)
                    nc.scalar.activation(ps_v[:, oc, :], ps_v[:, oc, :], ACT.Tanh,
                                         bias=bias[:, BV, oc:oc + 1]).then_inc(v_ready, 1)

            def normalise(i, q):
                act.wait_ge(shift_ready[q], i + 1)
                for b in range(GB):
                    nc.scalar.activation(y[q][:, b, :], y[q][:, b, :], ACT.Identity, bias=shift[q][:, b:b + 1],
                                         scale=rstd[q][:, b:b + 1]).then_inc(normed[q], 1)

            def pair(i, carry):
                split_first_half(i, 0, carry)
                for j in range(FR):
                    q = j % SLOTS
                    before = carry or j > 0
                    if before:
                        tanh_v(i, j - 1)
                    if carry and j in (SLOTS, SLOTS + 1):
                        normalise(i - 1, j - SLOTS)
                    for oc in range(C):
                        if 0 < j < FR - 1:
                            act.wait_ge(h_ready, C * frames(i, j - 1) - 1 + oc)
                            nc.scalar.copy(hT_hi[:, oc, :], hT[1 - q][:, oc, :]).then_inc(hT_hi_ready, 1)
                        act.wait_ge(rsum_ready, C * frames(i, j) - 1 + oc)
                        nc.scalar.activation(ps_tr[:, oc, :], ps_tr[:, oc, :], ACT.Sigmoid,
                                             bias=bias[:, BR, oc:oc + 1]).then_inc(r_ready, 1)
                    for oc in range(C):
                        act.wait_ge(zpre_ready, C * frames(i, j) - 1 + oc)
                        if (carry or j >= SLOTS) and oc == 0:
                            act.wait_ge(zd_ready, C * frames(i, j - SLOTS))
                        nc.scalar.activation(z[q][:, oc, :], ps_uz[:, oc, :], ACT.Sigmoid,
                                             bias=bias[:, BZ, oc:oc + 1]).then_inc(z_ready, 1)
                        act.wait_ge(rh_ready, C * frames(i, j) - 1 + oc)
                        nc.scalar.copy(rh_hi[:, oc, :], rh[:, oc, :]).then_inc(rh_hi_ready, 1)
                    if j < FR - 1:
                        split_first_half(i, j + 1, carry)

            act.dma_start(square[0][:, :, :], u3_w.rearrange("(c p) i -> p c i", p=P)).then_inc(w_loaded[U3], DMA)
            act.dma_start(square[1][:, :, :], u5_w.rearrange("(c p) i -> p c i", p=P)).then_inc(w_loaded[U5], DMA)
            for n, b in enumerate((w3_b, u3_b, w4_b, w5_b, u5_b)):
                act.dma_start(bias_rows[C * n:C * (n + 1), :], b.rearrange("(c p) -> c p", p=P)).then_inc(bias_loaded, DMA)
            act.wait_ge(wt_transposed, 1)
            nc.scalar.copy(adjT[:, :], ps_tr[:, 1, 0:N]).then_inc(wt_hi_ready, 1)
            banks = [ps_v[:, 0, :], ps_v[:, 1, :], ps_a[:, 0, :], ps_a[:, 1, :], ps_tr[:, 0, :]]
            for n, k in enumerate((U3, W4, W3, W5, U5)):
                act.wait_ge(wt_transposed, n + 2)
                nc.scalar.copy(wt_hi[k][:, :, :], banks[k].rearrange("p (c o) -> p c o", c=C)).then_inc(wt_hi_ready, 1)
            act.wait_ge(bias_transposed, 1)
            nc.scalar.copy(bias_in[:, :, :],
                           ps_uz[:, 0, 0:5 * C].rearrange("p (n c) -> p n c", c=C)).then_inc(bias_copied, 1)
            act.wait_ge(bias_ready, 3)

            pair(0, False)
            with act.Fori(1, PAIRS) as i:
                pair(i, True)
            tanh_v(PAIRS - 1, FR - 1)
            for q in range(SLOTS):
                normalise(PAIRS - 1, q)

        @block.vector
        def _(dve):
            def residual(i, q, carry):
                dve.wait_ge(x_kept[q], i + 1)
                if carry:
                    dve.wait_ge(stored[q], DMA * i)
                for hf in range(2):
                    dve.wait_ge(h_out[q], 2 * i + hf + 1)
                    part = slice(hf * HB, (hf + 1) * HB)
                    nc.vector.tensor_tensor(y[q][:, part, :], by_batch(ps_tr[:, hf, :]), x_res[q][:, part, :],
                                            ALU.add).then_inc(y_ready[q], 1)

            def statistics(i, q):
                dve.wait_ge(y_ready[q], 2 * (i + 1))
                for b in range(GB):
                    nc.vector.bn_stats(stats[q][:, b, :], y[q][:, b, :]).then_inc(stats_ready[q], 1)
                dve.wait_ge(stats_ready[q], GB * (i + 1))
                dve.sem_inc(dve_passed, 1)
                for b in range(GB):
                    nc.vector.bn_aggr(meanvar[q][:, b, :], stats[q][:, b, :]).then_inc(meanvar_ready[q], 1)

            def split_first_half(i, j, carry, out_carry):
                q = j % SLOTS
                if j < SLOTS:
                    for c in range(C):
                        dve.wait_ge(hT_hi_ready, C * frames(i, j) - 1 + c)
                        nc.vector.tensor_tensor(hT_lo[:, c, :], ps_uz[:, c, :], f32(hT_hi[:, c, :]),
                                                ALU.subtract).then_inc(h0_lo_ready[q], 1)
                    if carry:
                        residual(i - 1, q, out_carry)
                for hf in range(2):
                    dve.wait_ge(a_hi_ready, 2 * frames(i, j) - 1 + hf)
                    nc.vector.tensor_tensor(half(aT_lo, hf), by_chunk(ps_a[:, hf, :]), f32(half(aT_hi, hf)),
                                            ALU.subtract).then_inc(a_lo_ready, 1)

            def v_minus_h(i, j, c):
                dve.wait_ge(v_ready, C * frames(i, j) - 1 + c)
                nc.vector.tensor_tensor(dz[:, c, :], ps_v[:, c, :], hT[j % SLOTS][:, c, :],
                                        ALU.subtract).then_inc(d_ready, 1)

            def times_z(i, j, c):
                dve.wait_ge(d_ready, C * frames(i, j) - 1 + c)
                nc.vector.tensor_tensor(dz[:, c, :], dz[:, c, :], z[j % SLOTS][:, c, :],
                                        ALU.mult).then_inc(zd_ready, 1)

            def new_h(i, j, c):
                dve.wait_ge(zd_ready, C * frames(i, j) - 1 + c)
                nc.vector.tensor_tensor(hT[j % SLOTS][:, c, :], dz[:, c, :], hT[j % SLOTS][:, c, :],
                                        ALU.add).then_inc(h_ready, 1)

            def add_u(i, j, c):
                dve.wait_ge(rpre_ready, C * frames(i, j) - 1 + c)
                dve.wait_ge(u_copied, C * frames(i, j) - 1 + c)
                nc.vector.tensor_tensor(ps_tr[:, c, :], ps_tr[:, c, :], u_sb[:, c, :],
                                        ALU.add).then_inc(rsum_ready, 1)

            def times_r(i, j, c):
                dve.wait_ge(r_ready, C * frames(i, j) - 1 + c)
                if j < SLOTS:
                    dve.wait_ge(h0_ready[j], C * i + c + 1)
                nc.vector.tensor_tensor(rh[:, c, :], ps_tr[:, c, :], hT[j % SLOTS][:, c, :],
                                        ALU.mult).then_inc(rh_ready, 1)

            def rh_low(i, j, c):
                dve.wait_ge(rh_hi_ready, C * frames(i, j) - 1 + c)
                nc.vector.tensor_tensor(rh_lo[:, c, :], rh[:, c, :], f32(rh_hi[:, c, :]),
                                        ALU.subtract).then_inc(rh_lo_ready, 1)

            def h_low(i, j, c):
                dve.wait_ge(hT_hi_ready, C * frames(i, j) - 1 + c)
                nc.vector.tensor_tensor(hT_lo[:, c, :], hT[j % SLOTS][:, c, :], f32(hT_hi[:, c, :]),
                                        ALU.subtract).then_inc(hT_lo_ready, 1)

            def pair(i, carry, out_carry):
                split_first_half(i, 0, carry, out_carry)
                for j in range(FR):
                    before = carry or j > 0
                    if before:
                        v_minus_h(i, j - 1, 0)
                        times_z(i, j - 1, 0)
                        v_minus_h(i, j - 1, 1)
                        new_h(i, j - 1, 0)
                        times_z(i, j - 1, 1)
                    add_u(i, j, 0)
                    if before:
                        new_h(i, j - 1, 1)
                    add_u(i, j, 1)
                    for c in range(C):
                        if 0 < j < FR - 1:
                            h_low(i, j + 1, c)
                        times_r(i, j, c)
                    rh_low(i, j, 0)
                    rh_low(i, j, 1)
                    if carry and j in (1, 2):
                        statistics(i - 1, j - 1)
                    if j < FR - 1:
                        split_first_half(i, j + 1, carry, out_carry)

            for k in (W4, W3, W5):
                dve.wait_ge(w_loaded[k], DMA)
                nc.vector.tensor_tensor(wsum[k][:, :, :], wide[k][:, :, 0:D], wide[k][:, :, D:2 * D],
                                        ALU.add).then_inc(wsum_ready, 1)
            banks = [ps_v[:, 0, :], ps_v[:, 1, :], ps_a[:, 0, :], ps_a[:, 1, :], ps_tr[:, 0, :]]
            for n, k in enumerate((U3, W4, W3, W5, U5)):
                dve.wait_ge(wt_hi_ready, n + 2)
                nc.vector.tensor_tensor(wt_lo[k][:, :, :], banks[k].rearrange("p (c o) -> p c o", c=C),
                                        f32(wt_hi[k][:, :, :]), ALU.subtract).then_inc(wt_lo_ready, 1)
            dve.wait_ge(bias_copied, 1)
            for b, (l, r) in ((BZ, (0, 1)), (BR, (2, 1)), (BV, (3, 4))):
                nc.vector.tensor_tensor(bias[:, b, :], bias_in[:, l, :], bias_in[:, r, :],
                                        ALU.add).then_inc(bias_ready, 1)

            pair(0, False, False)
            with dve.Fori(1, PAIRS) as i:
                pair(i, True, True)
            last = PAIRS - 1
            residual(last, 0, True)
            for c in range(C):
                v_minus_h(last, FR - 1, c)
                times_z(last, FR - 1, c)
                new_h(last, FR - 1, c)
            statistics(last, 0)
            residual(last, 1, True)
            statistics(last, 1)

        @block.gpsimd
        def _(pool):
            def keep_x(i, q, carry):
                pool.wait_ge(x_loaded[q], DMA * (i + 1))
                if carry:
                    pool.wait_ge(y_ready[q], 2 * i)
                if carry:
                    pool.sem_inc(pool_passed, 1)
                nc.gpsimd.tensor_copy(x_res[q][:, :, :], x_in[q][:, :, :]).then_inc(x_kept[q], 1)

            def scale_and_shift(i, q):
                pool.wait_ge(meanvar_ready[q], GB * (i + 1))
                pool.sem_inc(pool_passed, 1)
                nc.gpsimd.tensor_scalar(var_eps[q][:, :], meanvar[q][:, :, 1], EPS, None,
                                        ALU.add).then_inc(var_eps_ready[q], 1)
                nc.gpsimd.tensor_scalar(neg_mean[q][:, :], meanvar[q][:, :, 0], -1.0, None,
                                        ALU.mult).then_inc(neg_mean_ready[q], 1)
                pool.wait_ge(var_eps_ready[q], i + 1)
                nc.gpsimd.tensor_tensor(rstd[q][:, :], var_eps[q][:, :], neg_half[:, :],
                                        ALU.pow).then_inc(rstd_ready[q], 1)
                pool.wait_ge(rstd_ready[q], i + 1)
                pool.wait_ge(neg_mean_ready[q], i + 1)
                nc.gpsimd.tensor_tensor(shift[q][:, :], neg_mean[q][:, :], rstd[q][:, :],
                                        ALU.mult).then_inc(shift_ready[q], 1)

            def pair(i, carry):
                for q in range(SLOTS):
                    if carry:
                        scale_and_shift(i - 1, q)
                for q in range(SLOTS):
                    keep_x(i, q, carry)

            nc.gpsimd.memset(ident[:, :], 0.0).then_inc(ident_zero, 1)
            pool.wait_ge(ident_zero, 1)
            nc.gpsimd.affine_select(out=ident[:, :], in_=ident[:, :], compare_op=ALU.not_equal, fill=1.0,
                                    base=0, pattern=[[-1, P]], channel_multiplier=1).then_inc(ident_ready, 1)
            nc.gpsimd.memset(neg_half[:, :], -0.5).then_inc(neg_half_ready, 1)
            pool.wait_ge(neg_half_ready, 1)

            pair(0, False)
            with pool.Fori(1, PAIRS) as i:
                pair(i, True)
            scale_and_shift(PAIRS - 1, 0)
            scale_and_shift(PAIRS - 1, 1)


_INS = ["x", "adj", "L0_gnn_w3_w", "L0_gnn_w3_b", "L0_gnn_u3_w", "L0_gnn_u3_b", "L0_gnn_w4_w", "L0_gnn_w4_b",
        "L0_gnn_w5_w", "L0_gnn_w5_b", "L0_gnn_u5_w", "L0_gnn_u5_b"]


def kernel(**inputs):
    import numpy as np
    import concourse.bacc as bacc
    from concourse.bass_utils import run_bass_kernel_spmd

    nc = bacc.Bacc("TRN2", target_bir_lowering=False, num_devices=1)
    arrays, args = {}, []
    for name in _INS:
        a = np.ascontiguousarray(inputs[name])
        arrays[f"in_{name}"] = a
        args.append(nc.dram_tensor(f"in_{name}", a.shape, mybir.dt.from_np(a.dtype), kind="ExternalInput").ap())
    args.append(nc.dram_tensor("out", inputs["x"].shape, F32, kind="ExternalOutput").ap())
    build(nc, *args)
    result = run_bass_kernel_spmd(nc, [arrays], core_ids=[0])
    return result.results[0]["out"]
```

```python
from contextlib import ExitStack

import concourse.bass as bass
from concourse import mybir

F32 = mybir.dt.float32
F32R = mybir.dt.float32r
ALU = mybir.AluOpType
ACT = mybir.ActivationFunctionType

STEPS = 3
SLOTS = 4
P = 128
EPS = 1e-5


def build(nc, x, adj, w3_w, w3_b, u3_w, u3_b, w4_w, w4_b, w5_w, w5_b, u5_w, u5_b, out):
    B, N, D = x.shape
    ROWS = 512
    GB = ROWS // N
    C = D // P
    HB = GB // 2
    HALF = ROWS // 2
    FR = STEPS * SLOTS
    ROUNDS = B // (GB * SLOTS)
    BLK = 32
    QUADS = P // BLK
    NBLK = ROWS // BLK
    DMA = 16
    assert N == P and C == 2 and GB == 4 and ROUNDS * GB * SLOTS == B

    x_rows = x.rearrange("b n d -> n b d")
    x_blocks = x.rearrange("b n d -> (b n) d").rearrange("(k r) (c q f) -> q r c k f", r=BLK, c=C, f=BLK)
    out_rows = out.rearrange("b n d -> n b d")

    ctx = ExitStack()
    with ctx:
        def sb(name, shape, dt=F32):
            return ctx.enter_context(nc.sbuf_tensor(name, shape, dt))

        def ps(name):
            return ctx.enter_context(nc.psum_tensor(name, [P, 2, ROWS], F32))

        def sem(name):
            return ctx.enter_context(nc.semaphore(name))

        ident = sb("ident", [P, P])
        neg_half = sb("neg_half", [P, GB])
        wide = [sb(f"wide{k}", [P, C, 2 * D]) for k in range(3)]
        square = [sb(f"square{k}", [P, C, D]) for k in range(2)]
        wsum = [sb(f"wsum{k}", [P, C, D]) for k in range(3)]
        table_probe = sb("table_probe", [P, GB])
        adj_in = sb("adj_in", [P, N])
        bias_rows = sb("bias_rows", [5 * C, P])
        bias_in = sb("bias_in", [P, 5, C])
        bias = sb("bias", [P, 3, C])
        wt_hi = [sb(f"wt_hi{k}", [P, C, D], F32R) for k in range(5)]
        wt_lo = [sb(f"wt_lo{k}", [P, C, D], F32R) for k in range(5)]
        adjT = sb("adjT", [P, N])
        W3, W4, W5, U3, U5 = range(5)
        BZ, BR, BV = range(3)

        xT = [sb(f"xT{q}", [P, C, ROWS]) for q in range(SLOTS)]
        hT = [sb(f"hT{q}", [P, C, ROWS]) for q in range(SLOTS)]
        hn = [sb(f"hn{q}", [P, C, GB, P]) for q in range(SLOTS)]
        stats = [sb(f"stats{q}", [P, GB, 6]) for q in range(SLOTS)]
        meanvar = [sb(f"meanvar{q}", [P, GB, 2]) for q in range(SLOTS)]
        var_eps = [sb(f"var_eps{q}", [P, GB]) for q in range(SLOTS)]
        neg_mean = [sb(f"neg_mean{q}", [P, GB]) for q in range(SLOTS)]
        rstd = [sb(f"rstd{q}", [P, GB]) for q in range(SLOTS)]
        shift = [sb(f"shift{q}", [P, GB]) for q in range(SLOTS)]

        x_in = [sb(f"x_in{k}", [P, GB, D]) for k in range(2)]
        x_blk = [sb(f"x_blk{k}", [P, C, NBLK, BLK]) for k in range(2)]
        hb = [sb(f"hb{k}", [P, C, GB, QUADS, BLK]) for k in range(2)]
        z = [sb(f"z{k}", [P, C, ROWS]) for k in range(2)]
        y = [sb(f"y{k}", [P, GB, D]) for k in range(2)]

        hT_hi = sb("hT_hi", [P, C, ROWS], F32R)
        hT_lo = sb("hT_lo", [P, C, ROWS], F32R)
        aT_hi = sb("aT_hi", [P, C, ROWS], F32R)
        aT_lo = sb("aT_lo", [P, C, ROWS], F32R)
        u_sb = sb("u_sb", [P, C, ROWS])
        rh = sb("rh", [P, C, ROWS])
        rh_hi = sb("rh_hi", [P, C, ROWS], F32R)
        rh_lo = sb("rh_lo", [P, C, ROWS], F32R)
        dz = sb("dz", [P, C, ROWS])

        ps_v, ps_uz, ps_a, ps_r = ps("ps_v"), ps("ps_uz"), ps("ps_a"), ps("ps_r")

        def f32(t):
            return t.bitcast(F32)

        def half(t, h):
            return t[:, :, h * HALF:(h + 1) * HALF]

        def by_chunk(bank):
            return bank.rearrange("p (c r) -> p c r", c=C)

        def by_batch(bank):
            return bank.rearrange("p (b d) -> p b d", b=HB)

        w_loaded = [sem(f"w_loaded{k}") for k in range(5)]
        adj_loaded, bias_loaded = sem("adj_loaded"), sem("bias_loaded")
        ident_zero, ident_ready, neg_half_ready = sem("ident_zero"), sem("ident_ready"), sem("neg_half_ready")
        adjT_ready = sem("adjT_ready")
        wsum_ready, bias_ready = sem("wsum_ready"), sem("bias_ready")
        bias_transposed, bias_copied = sem("bias_transposed"), sem("bias_copied")
        adj_transposed = sem("adj_transposed")
        wt_transposed, wt_hi_ready, wt_lo_ready = sem("wt_transposed"), sem("wt_hi_ready"), sem("wt_lo_ready")

        x_loaded = [sem(f"x_loaded{k}") for k in range(2)]
        blocks_loaded = [sem(f"blocks_loaded{k}") for k in range(2)]
        stored = [sem(f"stored{k}") for k in range(2)]

        xT_ready = [sem(f"xT_ready{q}") for q in range(SLOTS)]
        xh_ready = [sem(f"xh_ready{q}") for q in range(SLOTS)]
        moved = [sem(f"moved{q}") for q in range(SLOTS)]
        stats_ready = [sem(f"stats_ready{q}") for q in range(SLOTS)]
        meanvar_ready = [sem(f"meanvar_ready{q}") for q in range(SLOTS)]
        var_eps_ready = [sem(f"var_eps_ready{q}") for q in range(SLOTS)]
        neg_mean_ready = [sem(f"neg_mean_ready{q}") for q in range(SLOTS)]
        rstd_ready = [sem(f"rstd_ready{q}") for q in range(SLOTS)]
        shift_ready = [sem(f"shift_ready{q}") for q in range(SLOTS)]
        normed = [sem(f"normed{q}") for q in range(SLOTS)]

        hb_ready = sem("hb_ready")
        y_transposed = sem("y_transposed")

        hT_hi_ready = sem("hT_hi_ready")
        hT_lo_ready = sem("hT_lo_ready")
        a_ready = sem("a_ready")
        a_hi_ready = sem("a_hi_ready")
        a_lo_ready = sem("a_lo_ready")
        u_ready = sem("u_ready")
        u_copied = sem("u_copied")
        rpre_ready = sem("rpre_ready")
        rsum_ready = sem("rsum_ready")
        r_ready = sem("r_ready")
        zpre_ready = sem("zpre_ready")
        z_ready = sem("z_ready")
        rh_ready = sem("rh_ready")
        rh_hi_ready = sem("rh_hi_ready")
        rh_lo_ready = sem("rh_lo_ready")
        vpre_ready = sem("vpre_ready")
        v_ready = sem("v_ready")
        d_ready = sem("d_ready")
        zd_ready = sem("zd_ready")
        h_ready = sem("h_ready")

        pool_passed, dve_passed = sem("pool_passed"), sem("dve_passed")

        def frames(i, j):
            return FR * i + (j + 1)

        def moves(i, j):
            return QUADS ** 2 * DMA * (STEPS * i + j // SLOTS + 1)

        def turn(i, q):
            return SLOTS // 2 * i + (q // 2 + 1)

        def frame_before(i, j):
            return (i, j - 1) if j > 0 else (i - 1, FR - 1)

        def h_of(j):
            return xT[j] if j < SLOTS else hT[j % SLOTS]

        PREPARED = (U3, W4, W3, U5, W5)
        wt_bank = {U3: ps_r[:, 0, :], W4: ps_v[:, 0, :], W3: ps_v[:, 1, :], W5: ps_a[:, 0, :], U5: ps_a[:, 1, :]}
        adj_bank = ps_r[:, 1, 0:N]
        bias_bank = ps_r[:, 1, N:N + 5 * C]

        block = ctx.enter_context(nc.Block())

        @block.sync
        def _(sp):
            def load_blocks(i, q):
                for f in range(QUADS):
                    sp.dma_start(x_blk[q % 2][f * BLK:(f + 1) * BLK, :, :, :],
                                 x_blocks[f, :, :, bass.ds((SLOTS * i + q) * NBLK, NBLK), :])\
                      .then_inc(blocks_loaded[q % 2], DMA)

            def load_rows(i, q):
                sp.dma_start(x_in[q % 2][:, :, :],
                             x_rows[:, bass.ds((SLOTS * i + q) * GB, GB), :]).then_inc(x_loaded[q % 2], DMA)

            def load(i, q):
                oi, oq = (i, q - 2) if q >= 2 else (i - 1, q + 2)
                sp.wait_ge(xT_ready[oq], oi + 1)
                load_blocks(i, q)
                sp.wait_ge(a_ready, 2 * frames(oi, oq))
                load_rows(i, q)

            def move(i, j):
                sp.wait_ge(hb_ready, frames(i, j))
                for n in range(QUADS):
                    for f in range(QUADS):
                        sp.dma_start(hn[j % SLOTS][n * BLK:(n + 1) * BLK, :, :, f * BLK:(f + 1) * BLK],
                                     hb[j % 2][f * BLK:(f + 1) * BLK, :, :, n, :]).then_inc(moved[j % SLOTS], DMA)

            def store(i, q):
                sp.wait_ge(normed[q], GB * (i + 1))
                sp.dma_start(out_rows[:, bass.ds((SLOTS * i + q) * GB, GB), :],
                             y[q % 2][:, :, :]).then_inc(stored[q % 2], DMA)

            def frame(i, j, carry):
                if j < 2:
                    load(i, j + 2)
                if carry and j < SLOTS:
                    store(i - 1, j)
                if carry or j > 0:
                    move(*frame_before(i, j))

            for k in range(2):
                sp.sem_inc(stored[k], DMA)
            wide_in = [w3_w, w4_w, w5_w]
            sp.dma_start(adj_in[:, :], adj).then_inc(adj_loaded, DMA)
            load_rows(0, 0)
            load_blocks(0, 0)
            for k in (W4, W3, W5):
                sp.dma_start(wide[k][:, :, :],
                             wide_in[k].rearrange("(c p) i -> p c i", p=P)).then_inc(w_loaded[k], DMA)
                if k == W4:
                    for n, b in enumerate((w3_b, u3_b, w4_b, w5_b, u5_b)):
                        sp.dma_start(bias_rows[C * n:C * (n + 1), :],
                                     b.rearrange("(c p) -> c p", p=P)).then_inc(bias_loaded, DMA)
                if k == W3:
                    sp.dma_start(square[1][:, :, :], u5_w.rearrange("(c p) i -> p c i", p=P)).then_inc(w_loaded[U5], DMA)
            load_blocks(0, 1)
            load_rows(0, 1)

            EARLY = SLOTS
            for j in range(EARLY):
                frame(0, j, False)
            with sp.Fori(1, ROUNDS) as i:
                load(i, 0)
                load(i, 1)
                for j in range(EARLY, FR):
                    frame(i - 1, j, True)
                for j in range(EARLY):
                    frame(i, j, True)
            last = ROUNDS - 1
            for j in range(EARLY, FR - 1):
                frame(last, j, True)
            for q in range(SLOTS - 1):
                store(last, q)
            for hf in range(2):
                part = slice(hf * HB, (hf + 1) * HB)
                sp.wait_ge(normed[SLOTS - 1], GB * last + HB * (hf + 1))
                sp.dma_start(out_rows[:, B - GB + hf * HB:B - GB + (hf + 1) * HB, :],
                             y[1][:, part, :]).then_inc(stored[1], DMA)
            sp.wait_ge(stored[0], DMA * (SLOTS // 2 * ROUNDS + 1))
            sp.wait_ge(stored[1], DMA * (SLOTS // 2 * ROUNDS + 2))

        @block.tensor
        def _(pe):
            def product(dst, lhs_hi, lhs_lo, rhs_hi, rhs_lo, first, last):
                nc.tensor.matmul(dst, lhs_lo, rhs_hi, start=first, stop=False, skip_group_check=True)
                nc.tensor.matmul(dst, lhs_hi, rhs_lo, start=False, stop=False, skip_group_check=True)
                return nc.tensor.matmul(dst, lhs_hi, rhs_hi, start=False, stop=last, skip_group_check=True)

            def dense(dst, k, oc, hi, lo, start, stop):
                for kc in range(C):
                    cols = slice(oc * P, (oc + 1) * P)
                    done = product(dst[:, oc, :], wt_hi[k][:, kc, cols], wt_lo[k][:, kc, cols],
                                   hi[:, kc, :], lo[:, kc, :], start and kc == 0, stop and kc == C - 1)
                return done

            def aggregate(i, j):
                q = j % SLOTS
                if j < SLOTS:
                    pe.wait_ge(x_loaded[q % 2], DMA * turn(i, q))
                else:
                    pe.wait_ge(moved[q], moves(i, j - SLOTS))
                for hf in range(2):
                    bank = by_chunk(ps_a[:, hf, :])
                    for bb in range(HB):
                        b = hf * HB + bb
                        for c in range(C):
                            h_nodes = x_in[q % 2][:, b, c * P:(c + 1) * P] if j < SLOTS else hn[q][:, c, b, :]
                            done = nc.tensor.matmul(bank[:, c, bb * N:(bb + 1) * N], h_nodes,
                                                    adjT[:, :], start=True, stop=True)
                    done.then_inc(a_ready, 1)

            def u_product(i, j, between=None):
                pe.wait_ge(hT_hi_ready, C * frames(i, j))
                pe.wait_ge(hT_lo_ready, C * frames(i, j))
                for oc in range(C):
                    if between and oc == C - 1:
                        between(W4)
                    dense(ps_uz, U3, oc, hT_hi, hT_lo, True, True).then_inc(u_ready, 1)

            def first_half(i, j):
                aggregate(i, j)
                pe.wait_ge(z_ready, C * frames(*frame_before(i, j)))
                u_product(i, j)

            def gate_r(i, j):
                pe.wait_ge(a_hi_ready, 2 * frames(i, j))
                pe.wait_ge(a_lo_ready, 2 * frames(i, j))
                for oc in range(C):
                    dense(ps_r, W4, oc, aT_hi, aT_lo, True, True).then_inc(rpre_ready, 1)

            def gate_z(i, j):
                for oc in range(C):
                    pe.wait_ge(u_copied, C * frames(i, j) - 1 + oc)
                    dense(ps_uz, W3, oc, aT_hi, aT_lo, False, True).then_inc(zpre_ready, 1)

            def value(i, j, carry):
                for oc in range(C):
                    if carry or j > 0:
                        pe.wait_ge(d_ready, C * frames(*frame_before(i, j)) - 1 + oc)
                    dense(ps_v, W5, oc, aT_hi, aT_lo, True, False)

            def second_half(i, j, carry):
                gate_r(i, j)
                gate_z(i, j)
                value(i, j, carry)

            def candidate(i, j):
                pe.wait_ge(rh_hi_ready, C * frames(i, j))
                pe.wait_ge(rh_lo_ready, C * frames(i, j))
                for oc in range(C):
                    dense(ps_v, U5, oc, rh_hi, rh_lo, False, True).then_inc(vpre_ready, 1)

            def transpose_weight(k):
                if k in (U3, U5):
                    pe.wait_ge(w_loaded[k], DMA)
                    src = square[k - U3]
                else:
                    pe.wait_ge(wsum_ready, (W4, W3, W5).index(k) + 1)
                    src = wsum[k]
                dst = wt_bank[k].rearrange("p (c o) -> p c o", c=C)
                for kc in range(C):
                    for oc in range(C):
                        done = nc.tensor.transpose(dst[:, kc, oc * P:(oc + 1) * P],
                                                   src[:, oc, kc * P:(kc + 1) * P], ident[:, :])
                done.then_inc(wt_transposed, 1)

            def weight_ready(k):
                pe.wait_ge(wt_hi_ready, PREPARED.index(k) + 1)
                pe.wait_ge(wt_lo_ready, PREPARED.index(k) + 1)

            def keep_warm(n):
                for _ in range(n):
                    nc.tensor.transpose(ps_uz[:, 0, 0:P], ident[:, :], ident[:, :])

            def first_round():
                pe.wait_ge(ident_ready, 1)
                keep_warm(10)
                pe.wait_ge(adj_loaded, DMA)
                nc.tensor.transpose(adj_bank, adj_in[:, :], ident[:, :]).then_inc(adj_transposed, 1)
                transpose_weight(U3)
                pe.wait_ge(adjT_ready, 1)
                aggregate(0, 0)
                keep_warm(26)
                weight_ready(U3)
                u_product(0, 0, between=transpose_weight)
                pe.wait_ge(bias_loaded, 5 * DMA)
                nc.tensor.transpose(bias_bank, bias_rows[:, :],
                                    ident[0:5 * C, 0:5 * C]).then_inc(bias_transposed, 1)
                transpose_weight(W3)
                transpose_weight(U5)
                weight_ready(W4)
                pe.wait_ge(bias_copied, 1)
                gate_r(0, 0)
                transpose_weight(W5)
                weight_ready(W3)
                gate_z(0, 0)
                weight_ready(W5)
                value(0, 0, False)
                weight_ready(U5)
                first_half(0, 1)
                candidate(0, 0)
                for j in range(1, FR):
                    second_half(0, j, False)
                    if j < FR - 1:
                        first_half(0, j + 1)
                        candidate(0, j)

            first_round()
            with pe.Fori(1, ROUNDS) as i:
                first_half(i, 0)
                candidate(i - 1, FR - 1)
                for j in range(FR):
                    second_half(i, j, True)
                    if j < FR - 1:
                        first_half(i, j + 1)
                        candidate(i, j)

            def output(q, c, dst):
                for b in range(GB):
                    done = nc.tensor.transpose(by_batch(dst[:, b // HB, :])[:, b % HB, c * P:(c + 1) * P],
                                               hT[q][:, c, b * N:(b + 1) * N], ident[:, :])
                    if c == C - 1 and b % HB == HB - 1:
                        done.then_inc(y_transposed, 1)

            last = ROUNDS - 1
            pe.wait_ge(a_lo_ready, 2 * frames(last, FR - 1))
            for c in range(C):
                pe.wait_ge(h_ready, C * frames(last, FR - 2) - 1 + c)
                output(SLOTS - 2, c, ps_a)
            candidate(last, FR - 1)
            for c in range(C):
                pe.wait_ge(h_ready, C * frames(last, FR - 1) - 1 + c)
                output(SLOTS - 1, c, ps_r)

        @block.scalar
        def _(act):
            def split_first_half(i, j):
                for hf in range(2):
                    a_high(i, j, hf)
                copy_u(i, j)

            def a_high(i, j, hf):
                act.wait_ge(a_ready, 2 * frames(i, j) - 1 + hf)
                nc.scalar.copy(half(aT_hi, hf), by_chunk(ps_a[:, hf, :])).then_inc(a_hi_ready, 1)

            def h_high(i, j, c):
                if j < SLOTS:
                    act.wait_ge(xT_ready[j], i + 1)
                else:
                    act.wait_ge(h_ready, C * frames(i, j - SLOTS) - 1 + c)
                nc.scalar.copy(hT_hi[:, c, :], h_of(j)[:, c, :]).then_inc(hT_hi_ready, 1)

            def copy_u(i, j):
                for oc in range(C):
                    act.wait_ge(u_ready, C * frames(i, j) - 1 + oc)
                    nc.scalar.copy(u_sb[:, oc, :], ps_uz[:, oc, :]).then_inc(u_copied, 1)

            def tanh_v(i, j):
                for oc in range(C):
                    act.wait_ge(vpre_ready, C * frames(i, j) - 1 + oc)
                    nc.scalar.activation(ps_v[:, oc, :], ps_v[:, oc, :], ACT.Tanh,
                                         bias=bias[:, BV, oc:oc + 1]).then_inc(v_ready, 1)

            def normalise(i, q):
                act.wait_ge(shift_ready[q], i + 1)
                act.wait_ge(stored[q % 2], DMA * turn(i, q))
                for b in range(GB):
                    nc.scalar.activation(y[q % 2][:, b, :].rearrange("p (c f) -> p c f", c=C),
                                         hn[q][:, :, b, :], ACT.Identity, bias=shift[q][:, b:b + 1],
                                         scale=rstd[q][:, b:b + 1]).then_inc(normed[q], 1)

            def frame(i, j, carry, following):
                if carry or j > 0:
                    tanh_v(*frame_before(i, j))
                if j == FR - 1:
                    normalise(i, 0)
                elif carry and j < SLOTS - 1:
                    normalise(i - 1, j + 1)
                for oc in range(C):
                    if following:
                        h_high(*following, oc)
                    act.wait_ge(rsum_ready, C * frames(i, j) - 1 + oc)
                    nc.scalar.activation(ps_r[:, oc, :], ps_r[:, oc, :], ACT.Sigmoid,
                                         bias=bias[:, BR, oc:oc + 1]).then_inc(r_ready, 1)
                for oc in range(C):
                    act.wait_ge(zpre_ready, C * frames(i, j) - 1 + oc)
                    if (carry or j >= 2) and oc == 0:
                        act.wait_ge(zd_ready, C * frames(i, j - 2))
                    nc.scalar.activation(z[j % 2][:, oc, :], ps_uz[:, oc, :], ACT.Sigmoid,
                                         bias=bias[:, BZ, oc:oc + 1]).then_inc(z_ready, 1)
                    act.wait_ge(rh_ready, C * frames(i, j) - 1 + oc)
                    nc.scalar.copy(rh_hi[:, oc, :], rh[:, oc, :]).then_inc(rh_hi_ready, 1)
                if following:
                    split_first_half(*following)

            def weight_high(k):
                act.wait_ge(wt_transposed, PREPARED.index(k) + 1)
                nc.scalar.copy(wt_hi[k][:, :, :], wt_bank[k].rearrange("p (c o) -> p c o", c=C))\
                  .then_inc(wt_hi_ready, 1)

            act.dma_start(square[0][:, :, :], u3_w.rearrange("(c p) i -> p c i", p=P)).then_inc(w_loaded[U3], DMA)
            act.wait_ge(neg_half_ready, 1)
            nc.scalar.activation(table_probe[:, :], neg_half[:, :], ACT.Sigmoid)
            act.wait_ge(adj_transposed, 1)
            nc.scalar.copy(adjT[:, :], adj_bank).then_inc(adjT_ready, 1)
            weight_high(U3)
            for hf in range(2):
                a_high(0, 0, hf)
            for c in range(C):
                h_high(0, 0, c)
            weight_high(W4)
            copy_u(0, 0)
            act.wait_ge(bias_transposed, 1)
            nc.scalar.copy(bias_in[:, :, :], bias_bank.rearrange("p (n c) -> p n c", c=C)).then_inc(bias_copied, 1)
            weight_high(W3)
            weight_high(U5)
            weight_high(W5)
            act.wait_ge(bias_ready, 3)

            for j in range(FR - 1):
                frame(0, j, False, (0, j + 1))
            with act.Fori(1, ROUNDS) as i:
                frame(i - 1, FR - 1, False, (i, 0))
                for j in range(FR - 1):
                    frame(i, j, True, (i, j + 1))
            last = ROUNDS - 1
            frame(last, FR - 1, False, None)
            tanh_v(last, FR - 1)
            normalise(last, 1)
            q = SLOTS - 2
            act.wait_ge(shift_ready[q], ROUNDS)
            act.wait_ge(stored[0], DMA * turn(last, q))
            for b in range(GB):
                nc.scalar.activation(y[0][:, b, :], by_batch(ps_a[:, b // HB, :])[:, b % HB, :], ACT.Identity,
                                     bias=shift[q][:, b:b + 1], scale=rstd[q][:, b:b + 1]).then_inc(normed[q], 1)
            q = SLOTS - 1
            act.wait_ge(stored[1], DMA * turn(last, q))
            for hf in range(2):
                act.wait_ge(shift_ready[q], last + 1 + hf)
                for b in range(hf * HB, (hf + 1) * HB):
                    nc.scalar.activation(y[1][:, b, :], by_batch(ps_r[:, hf, :])[:, b % HB, :], ACT.Identity,
                                         bias=shift[q][:, b:b + 1], scale=rstd[q][:, b:b + 1]).then_inc(normed[q], 1)

        @block.vector
        def _(dve):
            def statistics(i, q):
                dve.wait_ge(moved[q], moves(i, FR - SLOTS + q))
                for b in range(GB):
                    nc.vector.bn_stats(stats[q][:, b, :], hn[q][:, :, b, :]).then_inc(stats_ready[q], 1)
                dve.wait_ge(stats_ready[q], GB * (i + 1))
                dve.sem_inc(dve_passed, 1)
                for b in range(GB):
                    nc.vector.bn_aggr(meanvar[q][:, b, :], stats[q][:, b, :]).then_inc(meanvar_ready[q], 1)

            def transpose_x(i, q):
                dve.wait_ge(blocks_loaded[q % 2], QUADS * DMA * turn(i, q))
                nc.vector.transpose(xT[q][:, :, :].rearrange("p c r -> p (c r)"),
                                    x_blk[q % 2][:, :, :, :].rearrange("p c k f -> p (c k f)")).then_inc(xT_ready[q], 1)

            def transpose_blocks(i, j, again):
                dve.wait_ge(h_ready, C * frames(i, j))
                if again:
                    bi, bj = (i, j - 2) if j >= 2 else (i - 1, j - 2 + FR)
                    dve.wait_ge(moved[bj % SLOTS], moves(bi, bj))
                nc.vector.transpose(hb[j % 2][:, :, :, :, :].rearrange("p c b n f -> p (c b n f)"),
                                    hT[j % SLOTS][:, :, :].rearrange("p c r -> p (c r)")).then_inc(hb_ready, 1)

            def a_low(i, j, hf):
                dve.wait_ge(a_hi_ready, 2 * frames(i, j) - 1 + hf)
                nc.vector.tensor_tensor(half(aT_lo, hf), by_chunk(ps_a[:, hf, :]), f32(half(aT_hi, hf)),
                                        ALU.subtract).then_inc(a_lo_ready, 1)

            def v_minus_h(i, j, c):
                dve.wait_ge(v_ready, C * frames(i, j) - 1 + c)
                nc.vector.tensor_tensor(dz[:, c, :], ps_v[:, c, :], h_of(j)[:, c, :],
                                        ALU.subtract).then_inc(d_ready, 1)

            def times_z(i, j, c):
                dve.wait_ge(d_ready, C * frames(i, j) - 1 + c)
                nc.vector.tensor_tensor(dz[:, c, :], dz[:, c, :], z[j % 2][:, c, :],
                                        ALU.mult).then_inc(zd_ready, 1)

            def new_h(i, j, c):
                dve.wait_ge(zd_ready, C * frames(i, j) - 1 + c)
                base = h_of(j)
                if j >= FR - SLOTS:
                    base = xT[j % SLOTS]
                    dve.wait_ge(xh_ready[j % SLOTS], i + 1)
                nc.vector.tensor_tensor(hT[j % SLOTS][:, c, :], dz[:, c, :], base[:, c, :],
                                        ALU.add).then_inc(h_ready, 1)

            def add_u(i, j, c):
                dve.wait_ge(rpre_ready, C * frames(i, j) - 1 + c)
                dve.wait_ge(u_copied, C * frames(i, j) - 1 + c)
                nc.vector.tensor_tensor(ps_r[:, c, :], ps_r[:, c, :], u_sb[:, c, :],
                                        ALU.add).then_inc(rsum_ready, 1)

            def times_r(i, j, c):
                dve.wait_ge(r_ready, C * frames(i, j) - 1 + c)
                nc.vector.tensor_tensor(rh[:, c, :], ps_r[:, c, :], h_of(j)[:, c, :],
                                        ALU.mult).then_inc(rh_ready, 1)

            def rh_low(i, j, c):
                dve.wait_ge(rh_hi_ready, C * frames(i, j) - 1 + c)
                nc.vector.tensor_tensor(rh_lo[:, c, :], rh[:, c, :], f32(rh_hi[:, c, :]),
                                        ALU.subtract).then_inc(rh_lo_ready, 1)

            def h_low(i, j, c):
                dve.wait_ge(hT_hi_ready, C * frames(i, j) - 1 + c)
                nc.vector.tensor_tensor(hT_lo[:, c, :], h_of(j)[:, c, :], f32(hT_hi[:, c, :]),
                                        ALU.subtract).then_inc(hT_lo_ready, 1)

            def frame(i, j, carry, following):
                before = carry or j > 0
                if following and following[1] < SLOTS and (carry or j > 0):
                    transpose_x(*following)
                if before:
                    bi, bj = frame_before(i, j)
                    v_minus_h(bi, bj, 0)
                    times_z(bi, bj, 0)
                    v_minus_h(bi, bj, 1)
                    new_h(bi, bj, 0)
                    times_z(bi, bj, 1)
                add_u(i, j, 0)
                if before:
                    new_h(bi, bj, 1)
                add_u(i, j, 1)
                for c in range(C):
                    if following:
                        h_low(*following, c)
                    times_r(i, j, c)
                rh_low(i, j, 0)
                rh_low(i, j, 1)
                if before and following:
                    transpose_blocks(bi, bj, carry or bj >= 2)
                if j >= FR - 2:
                    statistics(i, j - (FR - 2))
                elif carry and j < SLOTS - 2:
                    statistics(i - 1, j + 2)
                if following:
                    for hf in range(2):
                        a_low(*following, hf)

            def sum_halves(k):
                dve.wait_ge(w_loaded[k], DMA)
                nc.vector.tensor_tensor(wsum[k][:, :, :], wide[k][:, :, 0:D], wide[k][:, :, D:2 * D],
                                        ALU.add).then_inc(wsum_ready, 1)

            def weight_low(k):
                dve.wait_ge(wt_hi_ready, PREPARED.index(k) + 1)
                nc.vector.tensor_tensor(wt_lo[k][:, :, :], wt_bank[k].rearrange("p (c o) -> p c o", c=C),
                                        f32(wt_hi[k][:, :, :]), ALU.subtract).then_inc(wt_lo_ready, 1)

            weight_low(U3)
            transpose_x(0, 0)
            for c in range(C):
                h_low(0, 0, c)
            sum_halves(W4)
            for hf in range(2):
                a_low(0, 0, hf)
            weight_low(W4)
            sum_halves(W3)
            dve.wait_ge(bias_copied, 1)
            for b, (l, r) in ((BZ, (0, 1)), (BR, (2, 1)), (BV, (3, 4))):
                nc.vector.tensor_tensor(bias[:, b, :], bias_in[:, l, :], bias_in[:, r, :],
                                        ALU.add).then_inc(bias_ready, 1)
            weight_low(W3)
            sum_halves(W5)
            weight_low(U5)
            weight_low(W5)
            transpose_x(0, 1)

            for j in range(FR - 1):
                frame(0, j, False, (0, j + 1))
            with dve.Fori(1, ROUNDS) as i:
                frame(i - 1, FR - 1, True, (i, 0))
                for j in range(FR - 1):
                    frame(i, j, True, (i, j + 1))
            last = ROUNDS - 1
            frame(last, FR - 1, True, None)

            def last_statistics(q, src, hf):
                dve.wait_ge(y_transposed, 2 * (q - (SLOTS - 2)) + hf + 1)
                for b in range(hf * HB, (hf + 1) * HB):
                    nc.vector.bn_stats(stats[q][:, b, :],
                                       by_batch(src[:, hf, :])[:, b % HB, :]).then_inc(stats_ready[q], 1)
                dve.wait_ge(stats_ready[q], GB * last + HB * (hf + 1))
                for b in range(hf * HB, (hf + 1) * HB):
                    nc.vector.bn_aggr(meanvar[q][:, b, :], stats[q][:, b, :]).then_inc(meanvar_ready[q], 1)

            last_statistics(SLOTS - 2, ps_a, 0)
            last_statistics(SLOTS - 2, ps_a, 1)
            for c in range(C):
                v_minus_h(last, FR - 1, c)
                times_z(last, FR - 1, c)
                new_h(last, FR - 1, c)
            last_statistics(SLOTS - 1, ps_r, 0)
            last_statistics(SLOTS - 1, ps_r, 1)

        @block.gpsimd
        def _(pool):
            def add_x(i, q):
                pool.wait_ge(h_ready, C * frames(i, FR - 2 * SLOTS + q))
                nc.gpsimd.tensor_tensor(xT[q][:, :, :], xT[q][:, :, :], hT[q][:, :, :],
                                        ALU.add).then_inc(xh_ready[q], 1)

            def scale_and_shift(i, q, part=slice(0, GB), nth=1, in_loop=True):
                pool.wait_ge(meanvar_ready[q], GB * i + part.stop)
                if in_loop:
                    pool.sem_inc(pool_passed, 1)
                nc.gpsimd.tensor_scalar(var_eps[q][:, part], meanvar[q][:, part, 1], EPS, None,
                                        ALU.add).then_inc(var_eps_ready[q], 1)
                nc.gpsimd.tensor_scalar(neg_mean[q][:, part], meanvar[q][:, part, 0], -1.0, None,
                                        ALU.mult).then_inc(neg_mean_ready[q], 1)
                pool.wait_ge(var_eps_ready[q], i + nth)
                nc.gpsimd.tensor_tensor(rstd[q][:, part], var_eps[q][:, part], neg_half[:, part],
                                        ALU.pow).then_inc(rstd_ready[q], 1)
                pool.wait_ge(rstd_ready[q], i + nth)
                pool.wait_ge(neg_mean_ready[q], i + nth)
                nc.gpsimd.tensor_tensor(shift[q][:, part], neg_mean[q][:, part], rstd[q][:, part],
                                        ALU.mult).then_inc(shift_ready[q], 1)

            nc.gpsimd.memset(ident[:, :], 0.0).then_inc(ident_zero, 1)
            pool.wait_ge(ident_zero, 1)
            nc.gpsimd.affine_select(out=ident[:, :], in_=ident[:, :], compare_op=ALU.not_equal, fill=1.0,
                                    base=0, pattern=[[-1, P]], channel_multiplier=1).then_inc(ident_ready, 1)
            nc.gpsimd.memset(neg_half[:, :], -0.5).then_inc(neg_half_ready, 1)
            pool.wait_ge(neg_half_ready, 1)

            for q in range(SLOTS):
                add_x(0, q)
            with pool.Fori(1, ROUNDS) as i:
                for q in range(SLOTS):
                    scale_and_shift(i - 1, q)
                for q in range(SLOTS):
                    add_x(i, q)
            last = ROUNDS - 1
            for q in range(SLOTS - 1):
                scale_and_shift(last, q, in_loop=False)
            for hf in range(2):
                scale_and_shift(last, SLOTS - 1, slice(hf * HB, (hf + 1) * HB), hf + 1, in_loop=False)


_INS = ["x", "adj", "L0_gnn_w3_w", "L0_gnn_w3_b", "L0_gnn_u3_w", "L0_gnn_u3_b", "L0_gnn_w4_w", "L0_gnn_w4_b",
        "L0_gnn_w5_w", "L0_gnn_w5_b", "L0_gnn_u5_w", "L0_gnn_u5_b"]


def kernel(**inputs):
    import numpy as np
    import concourse.bacc as bacc
    from concourse.bass_utils import run_bass_kernel_spmd

    nc = bacc.Bacc("TRN2", target_bir_lowering=False, num_devices=1)
    arrays, args = {}, []
    for name in _INS:
        a = np.ascontiguousarray(inputs[name])
        arrays[f"in_{name}"] = a
        args.append(nc.dram_tensor(f"in_{name}", a.shape, mybir.dt.from_np(a.dtype), kind="ExternalInput").ap())
    args.append(nc.dram_tensor("out", inputs["x"].shape, F32, kind="ExternalOutput").ap())
    build(nc, *args)
    result = run_bass_kernel_spmd(nc, [arrays], core_ids=[0])
    return result.results[0]["out"]
```
